# Optimizing a Trainium2 kernel written in Bass

```python
import numpy as np
import jax
import jax.numpy as jnp

def _softmax(x, axis=-1):
    return jax.nn.softmax(x, axis=axis)

def _gelu(x):
    return jax.nn.gelu(x, approximate=True)

def _silu(x):
    return jax.nn.silu(x)

def _sigmoid(x):
    return jax.nn.sigmoid(x)

def _layernorm(x, axis=-1, eps=1e-05):
    m = jnp.mean(x, axis=axis, keepdims=True)
    v = jnp.var(x, axis=axis, keepdims=True)
    return (x - m) / jnp.sqrt(v + eps)

def _scatter_add(tgt, idx, src, axis=0):
    return tgt.at[idx].add(src)

def _segment_sum(src, seg, n):
    return jax.ops.segment_sum(src, seg, n)
kernel_name = 'mk_dlrm_tower_d1_rec_r8_a15af1'

def setup_inputs(seed: int=0):
    np.random.seed(seed)
    _w = jnp.asarray

    def _rec_inputs():
        import jax
        import jax.numpy as jnp
        _tk = jax.random.key(seed)
        ids = jnp.stack([jax.random.randint(jax.random.fold_in(_tk, 200 + f), (2048,), 0, v, jnp.int32) for f, v in enumerate([1250, 1000, 1250, 1000, 12500, 12500, 12500, 12500, 125000, 12500, 1250, 1000, 12500, 1250, 1000, 12500, 12500, 12500, 1000, 1000, 1000, 1000, 1000, 1000, 1000, 1000])], axis=1)
        tbl_0 = 0.05 * jax.random.normal(jax.random.fold_in(_tk, 500 + 0), (1250, 128), jnp.float32)
        tbl_1 = 0.05 * jax.random.normal(jax.random.fold_in(_tk, 500 + 1), (1000, 128), jnp.float32)
        tbl_2 = 0.05 * jax.random.normal(jax.random.fold_in(_tk, 500 + 2), (1250, 128), jnp.float32)
        tbl_3 = 0.05 * jax.random.normal(jax.random.fold_in(_tk, 500 + 3), (1000, 128), jnp.float32)
        tbl_4 = 0.05 * jax.random.normal(jax.random.fold_in(_tk, 500 + 4), (12500, 128), jnp.float32)
        tbl_5 = 0.05 * jax.random.normal(jax.random.fold_in(_tk, 500 + 5), (12500, 128), jnp.float32)
        tbl_6 = 0.05 * jax.random.normal(jax.random.fold_in(_tk, 500 + 6), (12500, 128), jnp.float32)
        tbl_7 = 0.05 * jax.random.normal(jax.random.fold_in(_tk, 500 + 7), (12500, 128), jnp.float32)
        tbl_8 = 0.05 * jax.random.normal(jax.random.fold_in(_tk, 500 + 8), (125000, 128), jnp.float32)
        tbl_9 = 0.05 * jax.random.normal(jax.random.fold_in(_tk, 500 + 9), (12500, 128), jnp.float32)
        tbl_10 = 0.05 * jax.random.normal(jax.random.fold_in(_tk, 500 + 10), (1250, 128), jnp.float32)
        tbl_11 = 0.05 * jax.random.normal(jax.random.fold_in(_tk, 500 + 11), (1000, 128), jnp.float32)
        tbl_12 = 0.05 * jax.random.normal(jax.random.fold_in(_tk, 500 + 12), (12500, 128), jnp.float32)
        tbl_13 = 0.05 * jax.random.normal(jax.random.fold_in(_tk, 500 + 13), (1250, 128), jnp.float32)
        tbl_14 = 0.05 * jax.random.normal(jax.random.fold_in(_tk, 500 + 14), (1000, 128), jnp.float32)
        tbl_15 = 0.05 * jax.random.normal(jax.random.fold_in(_tk, 500 + 15), (12500, 128), jnp.float32)
        tbl_16 = 0.05 * jax.random.normal(jax.random.fold_in(_tk, 500 + 16), (12500, 128), jnp.float32)
        tbl_17 = 0.05 * jax.random.normal(jax.random.fold_in(_tk, 500 + 17), (12500, 128), jnp.float32)
        tbl_18 = 0.05 * jax.random.normal(jax.random.fold_in(_tk, 500 + 18), (1000, 128), jnp.float32)
        tbl_19 = 0.05 * jax.random.normal(jax.random.fold_in(_tk, 500 + 19), (1000, 128), jnp.float32)
        tbl_20 = 0.05 * jax.random.normal(jax.random.fold_in(_tk, 500 + 20), (1000, 128), jnp.float32)
        tbl_21 = 0.05 * jax.random.normal(jax.random.fold_in(_tk, 500 + 21), (1000, 128), jnp.float32)
        tbl_22 = 0.05 * jax.random.normal(jax.random.fold_in(_tk, 500 + 22), (1000, 128), jnp.float32)
        tbl_23 = 0.05 * jax.random.normal(jax.random.fold_in(_tk, 500 + 23), (1000, 128), jnp.float32)
        tbl_24 = 0.05 * jax.random.normal(jax.random.fold_in(_tk, 500 + 24), (1000, 128), jnp.float32)
        tbl_25 = 0.05 * jax.random.normal(jax.random.fold_in(_tk, 500 + 25), (1000, 128), jnp.float32)
        _rk = jax.random.fold_in(_tk, 7)
        r_dense_features = -0.000520686 + 1.00062 * jax.random.normal(jax.random.fold_in(_rk, 101), (2048, 128), jnp.float32)
        W_top1 = 0.0405887 * jax.random.normal(jax.random.fold_in(_tk, 801), (607, 512), jnp.float32)
        W_top2 = 0.0441942 * jax.random.normal(jax.random.fold_in(_tk, 802), (512, 256), jnp.float32)
        W_top3 = 0.0625 * jax.random.normal(jax.random.fold_in(_tk, 803), (256, 1), jnp.float32)
        b_top1 = jnp.zeros((512,), jnp.float32)
        b_top2 = jnp.zeros((256,), jnp.float32)
        return (r_dense_features, ids, tbl_0, tbl_1, tbl_2, tbl_3, tbl_4, tbl_5, tbl_6, tbl_7, tbl_8, tbl_9, tbl_10, tbl_11, tbl_12, tbl_13, tbl_14, tbl_15, tbl_16, tbl_17, tbl_18, tbl_19, tbl_20, tbl_21, tbl_22, tbl_23, tbl_24, tbl_25, W_top1, b_top1, W_top2, b_top2, W_top3)
    r_dense_features, ids, tbl_0, tbl_1, tbl_2, tbl_3, tbl_4, tbl_5, tbl_6, tbl_7, tbl_8, tbl_9, tbl_10, tbl_11, tbl_12, tbl_13, tbl_14, tbl_15, tbl_16, tbl_17, tbl_18, tbl_19, tbl_20, tbl_21, tbl_22, tbl_23, tbl_24, tbl_25, W_top1, b_top1, W_top2, b_top2, W_top3 = _rec_inputs()

    def _L0_rec_setup():
        import jax, jax.numpy as jnp
        import numpy as np
        B, F, D = (2048, 26, 128)
        key = jax.random.key(seed)
        k1, k2 = jax.random.split(key)
        dense_features = jax.random.normal(k1, (B, D), dtype=jnp.float32)
        sparse_values = jax.random.normal(k2, (B, F, D), dtype=jnp.float32)
        return {'dense_features': dense_features, 'sparse_values': sparse_values}
    _L0_rec_all = _L0_rec_setup()
    _L0_rec_in = {k: v for k, v in _L0_rec_all.items() if k in ()}
    del _L0_rec_all
    return {'r_dense_features': r_dense_features, 'ids': ids, 'tbl_0': tbl_0, 'tbl_1': tbl_1, 'tbl_2': tbl_2, 'tbl_3': tbl_3, 'tbl_4': tbl_4, 'tbl_5': tbl_5, 'tbl_6': tbl_6, 'tbl_7': tbl_7, 'tbl_8': tbl_8, 'tbl_9': tbl_9, 'tbl_10': tbl_10, 'tbl_11': tbl_11, 'tbl_12': tbl_12, 'tbl_13': tbl_13, 'tbl_14': tbl_14, 'tbl_15': tbl_15, 'tbl_16': tbl_16, 'tbl_17': tbl_17, 'tbl_18': tbl_18, 'tbl_19': tbl_19, 'tbl_20': tbl_20, 'tbl_21': tbl_21, 'tbl_22': tbl_22, 'tbl_23': tbl_23, 'tbl_24': tbl_24, 'tbl_25': tbl_25, 'W_top1': W_top1, 'b_top1': b_top1, 'W_top2': W_top2, 'b_top2': b_top2, 'W_top3': W_top3}

def reference(r_dense_features, ids, tbl_0, tbl_1, tbl_2, tbl_3, tbl_4, tbl_5, tbl_6, tbl_7, tbl_8, tbl_9, tbl_10, tbl_11, tbl_12, tbl_13, tbl_14, tbl_15, tbl_16, tbl_17, tbl_18, tbl_19, tbl_20, tbl_21, tbl_22, tbl_23, tbl_24, tbl_25, W_top1, b_top1, W_top2, b_top2, W_top3):
    import jax
    import jax.numpy as jnp

    def _L0_rec_ref(dense_features, sparse_values):
        import jax, jax.numpy as jnp
        import numpy as np
        B, F, D = (2048, 26, 128)
        sd = jnp.einsum('bfd,bd->bf', sparse_values, dense_features)
        ss = jnp.einsum('bfd,bgd->bfg', sparse_values, sparse_values)
        iu, ju = jnp.triu_indices(F, k=1)
        pairs = ss[:, iu, ju]
        return jnp.concatenate([dense_features, sd, pairs], axis=1)
    e = jnp.stack([tbl_0[ids[:, 0]], tbl_1[ids[:, 1]], tbl_2[ids[:, 2]], tbl_3[ids[:, 3]], tbl_4[ids[:, 4]], tbl_5[ids[:, 5]], tbl_6[ids[:, 6]], tbl_7[ids[:, 7]], tbl_8[ids[:, 8]], tbl_9[ids[:, 9]], tbl_10[ids[:, 10]], tbl_11[ids[:, 11]], tbl_12[ids[:, 12]], tbl_13[ids[:, 13]], tbl_14[ids[:, 14]], tbl_15[ids[:, 15]], tbl_16[ids[:, 16]], tbl_17[ids[:, 17]], tbl_18[ids[:, 18]], tbl_19[ids[:, 19]], tbl_20[ids[:, 20]], tbl_21[ids[:, 21]], tbl_22[ids[:, 22]], tbl_23[ids[:, 23]], tbl_24[ids[:, 24]], tbl_25[ids[:, 25]]], axis=1)
    z = _L0_rec_ref(r_dense_features, e)
    z = z.reshape(z.shape[0], -1)
    h = jnp.concatenate([z, r_dense_features], axis=1)
    h = jnp.maximum(h @ W_top1 + b_top1, 0.0)
    h = jnp.maximum(h @ W_top2 + b_top2, 0.0)
    y = h @ W_top3
    return y

_drawn_inputs = setup_inputs


def setup_inputs(seed=0):
    import zlib

    import numpy as np

    out = dict(_drawn_inputs(seed))
    spreads = {'b_top1': (0.0, 0.1), 'b_top2': (0.0, 0.1)}
    factors = {}
    for name, (base, spread) in spreads.items():
        noise = np.random.default_rng([zlib.crc32(name.encode()), seed]).standard_normal(out[name].shape)
        drawn = base * np.exp(spread * noise) if base else spread * noise
        out[name] = jnp.asarray(drawn.astype(out[name].dtype))
    for name, factor in factors.items():
        out[name] = (out[name] * factor).astype(out[name].dtype)
    return out
```

```python
from contextlib import ExitStack

import concourse.bass as bass
from concourse import mybir

ALU = mybir.AluOpType
ACT = mybir.ActivationFunctionType
F32 = mybir.dt.float32
F32R = mybir.dt.float32r
I32 = mybir.dt.int32

P = 128
U = 2
BS = U * P
NOH = 5
S = 4
K = P // S
PAD = 32
OH_BUFS = 3
BANK = 512


def last_use(n, per_block, buffers):
    if n >= buffers:
        return per_block + n - buffers + 1
    before = [m for m in range(per_block) if m % buffers == n % buffers]
    return before[-1] + 1


def build_dlrm_tower(nc, dense, ids, ids_t, tables, w1, b1, w2, b2, w3, out):
    B, D = dense.shape
    F = len(tables)
    TG = F - NOH
    NB = B // BS
    VOH = tables[TG].shape[0]
    NCH = 8
    CR = VOH // NCH
    NG = TG + 1
    GROUPS = [(g, min(g + 4, NG)) for g in range(0, NG, 4)]
    OGROUPS = [(g, min(g + 2, NOH)) for g in range(0, NOH, 2)]
    NGR, NOG = len(GROUPS), len(OGROUPS)
    TURNS = U * NGR + NOG
    TURN_AT = [0, NGR + NOG]
    OH_AT = NGR
    NPAIR = (F + 1) * F // 2
    PC = NPAIR // 3
    H1, H2 = w1.shape[1], w2.shape[1]
    N1, N2 = H1 // P, H2 // P
    SETS = BANK // PAD
    GB = K // SETS
    CPB = 4
    CGROUPS = [(c, min(c + CPB, F)) for c in range(0, F, CPB)]
    POSTS = len(CGROUPS) + 2
    assert D == P and NB * BS == B and CR * NCH == VOH and CR <= P and PC * 3 == NPAIR and PC <= P
    assert all(t.shape[0] == VOH for t in tables[TG:])
    pair_at = [c * F - c * (c - 1) // 2 for c in range(F + 1)]

    with ExitStack() as ctx:
        def sb(name, shape, dt=F32):
            return ctx.enter_context(nc.sbuf_tensor(name, shape, dt))

        def psum(name):
            return ctx.enter_context(nc.psum_tensor(name, [P, BANK], F32))

        def sem(name):
            return ctx.enter_context(nc.semaphore(name))

        ones = sb("ones", [P, P])
        ident = sb("ident", [P, P])
        row_of = sb("row_of", [P, NCH], I32)
        idx = [sb(f"idx{u}", [P, F], I32) for u in range(U)]
        rows = [sb(f"rows{u}", [P, NG, D]) for u in range(U)]
        ids_bc = sb("ids_bc", [P, NOH, BS], I32)
        onehot = [sb(f"onehot{i}", [P, NCH, BS], F32R) for i in range(OH_BUFS)]
        tbl_raw = [sb(f"tbl_raw{i}", [P, NCH, D]) for i in range(2)]
        tbl_hi = [sb(f"tbl_hi{i}", [P, NCH, D], F32R) for i in range(NOH)]
        tbl_lo = [sb(f"tbl_lo{i}", [P, NCH, D], F32R) for i in range(NOH)]
        slot_t = sb("slot_t", [P, U, P, PAD])
        gram = sb("gram", [P, F, U * K])
        pairs = sb("pairs", [U * K, S, NPAIR])
        pairs_t = sb("pairs_t", [PC, 3, BS])
        dense_t = sb("dense_t", [P, BS])
        h1 = sb("h1", [P, N1, BS])
        h2 = sb("h2", [P, N2, BS])
        y_row = sb("y_row", [1, BS])
        w_dense = sb("w_dense", [P, H1])
        w_dense2 = sb("w_dense2", [P, H1])
        w_pair = sb("w_pair", [PC, 3, H1])
        w2_sb = sb("w2_sb", [P, N1, H2])
        w3_sb = sb("w3_sb", [P, N2])
        b1_sb = sb("b1_sb", [P, N1])
        b2_sb = sb("b2_sb", [P, N2])

        turn_bank = [psum(f"turn_bank{i}") for i in range(2)]
        gram_bank = [psum(f"gram_bank{i}") for i in range(GB)]
        post_bank = [psum(f"post_bank{i}") for i in range(2)]
        mlp_bank = [psum(f"mlp_bank{i}") for i in range(2)]

        idx_landed = [sem(f"idx_landed{u}") for u in range(U)]
        dense_landed = [sem(f"dense_landed{u}") for u in range(U)]
        rows_landed = [[sem(f"rows_landed{u}_{g}") for g in range(NGR)] for u in range(U)]
        ids_bc_landed = sem("ids_bc_landed")
        tbl_landed = [sem(f"tbl_landed{i}") for i in range(2)]
        weights_landed = sem("weights_landed")
        out_stored = sem("out_stored")
        ones_made = sem("ones_made")
        consts_made = sem("consts_made")
        pads_made = sem("pads_made")
        w_dense_made = sem("w_dense_made")
        hi_made = sem("hi_made")
        lo_made = sem("lo_made")
        onehot_made = sem("onehot_made")
        turned = sem("turned")
        turn_copied = sem("turn_copied")
        dense_t_made = sem("dense_t_made")
        gram_made = sem("gram_made")
        gram_copied = sem("gram_copied")
        post_made = sem("post_made")
        post_copied = sem("post_copied")
        l1_made = sem("l1_made")
        h1_made = sem("h1_made")
        l2_made = sem("l2_made")
        h2_made = sem("h2_made")
        l3_made = sem("l3_made")
        y_made = sem("y_made")
        sp_passed = sem("sp_passed")
        pool_passed = sem("pool_passed")
        pe_passed = sem("pe_passed")

        block = ctx.enter_context(nc.Block())

        @block.sync
        def _(sp):
            def load_idx(b, u):
                sp.dma_start(idx[u][:], ids[bass.ds(b * BS + u * P, P), :]).then_inc(idx_landed[u], 16)

            def load_dense(b, u):
                sp.dma_start(rows[u][:, 0, :],
                             dense[bass.ds(b * BS + u * P, P), :]).then_inc(dense_landed[u], 16)

            def load_ids_bc(b):
                src = ids_t[TG:F, bass.ds(b * BS, BS)].partition_broadcast(P)
                sp.dma_start(ids_bc[:], src).then_inc(ids_bc_landed, 16)

            load_idx(0, 0)
            load_dense(0, 0)
            load_idx(0, 1)
            load_ids_bc(0)
            for i in range(NOH):
                if i >= 2:
                    sp.wait_ge(lo_made, i - 1)
                src = tables[TG + i].rearrange("(c p) d -> p c d", p=CR)
                sp.dma_start(tbl_raw[i % 2][0:CR], src).then_inc(tbl_landed[i % 2], 16)
            load_dense(0, 1)
            sp.dma_start(w_dense[:], w1[0:D, :]).then_inc(weights_landed, 16)
            sp.dma_start(w_dense2[:], w1[D + NPAIR:2 * D + NPAIR, :]).then_inc(weights_landed, 16)
            sp.dma_start(w_pair[:], w1[D:D + NPAIR, :].rearrange("(c p) n -> p c n", p=PC)).then_inc(weights_landed, 16)
            sp.dma_start(w2_sb[:], w2.rearrange("(k p) n -> p k n", p=P)).then_inc(weights_landed, 16)
            sp.dma_start(w3_sb[:], w3).then_inc(weights_landed, 16)
            sp.dma_start(b1_sb[:], b1).then_inc(weights_landed, 16)
            sp.dma_start(b2_sb[:], b2).then_inc(weights_landed, 16)
            with sp.Fori(1, NB) as b:
                sp.wait_ge(onehot_made, b * NOH)
                load_ids_bc(b)
                for u in range(U):
                    for g in range(NGR):
                        lo, hi = GROUPS[g]
                        sp.wait_ge(rows_landed[u][g], b * 16 * (hi - max(lo, 1)))
                        sp.sem_inc(sp_passed, 1)
                    load_idx(b, u)
                    sp.wait_ge(turned, (b - 1) * TURNS + TURN_AT[u] + 1)
                    load_dense(b, u)

        @block.gpsimd
        def _(pool):
            nc.gpsimd.memset(ones[:], 1.0).then_inc(ones_made, 1)
            pool.wait_ge(ones_made, 1)
            nc.gpsimd.affine_select(out=ident[:], in_=ones[:], compare_op=ALU.is_equal, fill=0.0, base=0,
                                    pattern=[[-1, P]], channel_multiplier=1).then_inc(consts_made, 1)
            nc.gpsimd.iota(row_of[:], pattern=[[CR, NCH]], base=0, channel_multiplier=1).then_inc(consts_made, 1)

            def gather(b, first):
                for u in range(U):
                    pool.wait_ge(idx_landed[u], (b + 1) * 16)
                    for g, (lo, hi) in enumerate(GROUPS):
                        if not first:
                            pool.wait_ge(turned, (b - 1) * TURNS + TURN_AT[u] + g + 1)
                            pool.sem_inc(pool_passed, 1)
                        for slot in range(max(lo, 1), hi):
                            t = slot - 1
                            nc.gpsimd.indirect_dma_start(
                                rows[u][:, slot, :], None, tables[t],
                                bass.IndirectOffsetOnAxis(ap=idx[u][:, t:t + 1], axis=0),
                            ).then_inc(rows_landed[u][g], 16)

            gather(0, True)
            with pool.Fori(1, NB) as b:
                gather(b, False)

        @block.tensor
        def _(pe):
            def turn_tile(b, u, first):
                for g, (lo, hi) in enumerate(GROUPS):
                    n = TURN_AT[u] + g
                    if lo == 0:
                        pe.wait_ge(dense_landed[u], (b + 1) * 16)
                    pe.wait_ge(rows_landed[u][g], (b + 1) * 16 * (hi - max(lo, 1)))
                    if not first or n >= 2:
                        pe.wait_ge(turn_copied, (b - 1) * TURNS + last_use(n, TURNS, 2))
                    for slot in range(lo, hi):
                        j = slot - lo
                        mm = nc.tensor.transpose(turn_bank[n % 2][:, j * P:(j + 1) * P],
                                                 rows[u][:, slot, :], ident[:])
                    mm.then_inc(turned, 1)

            def pick(b, first):
                for g, (lo, hi) in enumerate(OGROUPS):
                    n = OH_AT + g
                    pe.wait_ge(turn_copied, (b - 1) * TURNS + last_use(n, TURNS, 2))
                    for i in range(lo, hi):
                        pe.wait_ge(onehot_made, b * NOH + i + 1)
                        if first:
                            pe.wait_ge(lo_made, i + 1)
                        for c in range(NCH):
                            for part in (tbl_hi, tbl_lo):
                                mm = nc.tensor.matmul(
                                    turn_bank[n % 2][:, (i - lo) * BS:(i - lo + 1) * BS],
                                    part[i][0:CR, c, :], onehot[i % OH_BUFS][0:CR, c, :],
                                    start=(c == 0 and part is tbl_hi), stop=(c == NCH - 1 and part is tbl_lo))
                    mm.then_inc(turned, 1)

            def gram_tile(b, u, first):
                pe.wait_ge(turn_copied, b * TURNS + TURN_AT[u] + (NGR if u else NGR + NOG))
                for h in range(GB):
                    if not first or u:
                        pe.wait_ge(gram_copied, (b * U + u - 1) * GB + h + 1)
                    for k in range(SETS):
                        for s in range(S):
                            at = s * K + h * SETS + k
                            mm = nc.tensor.matmul(gram_bank[h][s * PAD:(s + 1) * PAD, k * PAD:k * PAD + F],
                                                  slot_t[:, u, at, :], slot_t[:, u, at, 0:F],
                                                  start=True, stop=True, tile_position=(0, s * PAD))
                    mm.then_inc(gram_made, 1)

            def turn_gram(b, first):
                pe.wait_ge(gram_copied, (b + 1) * U * GB)
                for n, (lo, hi) in enumerate(CGROUPS):
                    if not first or n >= 2:
                        pe.wait_ge(post_copied, (b - 1) * POSTS + last_use(n, POSTS, 2))
                        pe.sem_inc(pe_passed, 1)
                    for c in range(lo, hi):
                        mm = nc.tensor.transpose(post_bank[n % 2][0:U * K, (c - lo) * P:(c - lo + 1) * P],
                                                 gram[:, c, :], ident[:])
                    mm.then_inc(post_made, 1)

            def turn_pairs(b):
                pe.wait_ge(post_copied, b * POSTS + len(CGROUPS))
                pe.sem_inc(pe_passed, 1)
                for i, chunks in enumerate(((0, 1), (2,))):
                    n = len(CGROUPS) + i
                    for j, q in enumerate(chunks):
                        for s in range(S):
                            at = j * BS + s * U * K
                            mm = nc.tensor.transpose(post_bank[n % 2][0:PC, at:at + U * K],
                                                     pairs[:, s, q * PC:(q + 1) * PC], ident[0:U * K, 0:U * K])
                    mm.then_inc(post_made, 1)

            def layer1(b, first):
                if first:
                    pe.wait_ge(w_dense_made, 1)
                    pe.wait_ge(weights_landed, 7 * 16)
                pe.wait_ge(dense_t_made, b + 1)
                pe.wait_ge(post_copied, (b + 1) * POSTS)
                for n in range(N1):
                    if not first and n == 0:
                        pe.wait_ge(h2_made, b * N2)
                    if not first and n == 2:
                        pe.wait_ge(y_made, b)
                    dst = mlp_bank[n // 2][:, (n % 2) * BS:(n % 2 + 1) * BS]
                    nc.tensor.matmul(dst, w_dense[:, n * P:(n + 1) * P], dense_t[:], start=True, stop=False)
                    for q in range(3):
                        mm = nc.tensor.matmul(dst, w_pair[:, q, n * P:(n + 1) * P], pairs_t[:, q, :],
                                              start=False, stop=(q == 2))
                    if n % 2:
                        mm.then_inc(l1_made, 1)

            def layer2(b):
                for m in range(N2):
                    for k in range(N1):
                        if m == 0:
                            pe.wait_ge(h1_made, b * N1 + max(k, 1) + 1)
                        mm = nc.tensor.matmul(mlp_bank[0][:, m * BS:(m + 1) * BS],
                                              w2_sb[:, k, m * P:(m + 1) * P], h1[:, k, :],
                                              start=(k == 0), stop=(k == N1 - 1))
                mm.then_inc(l2_made, 1)

            def layer3(b):
                for k in range(N2):
                    pe.wait_ge(h2_made, b * N2 + k + 1)
                    mm = nc.tensor.matmul(mlp_bank[1][0:1, 0:BS], w3_sb[:, k:k + 1], h2[:, k, :],
                                          start=(k == 0), stop=(k == N2 - 1))
                mm.then_inc(l3_made, 1)

            pe.wait_ge(consts_made, 1)
            turn_tile(0, 0, True)
            pick(0, True)
            pe.wait_ge(pads_made, 1)
            gram_tile(0, 0, True)
            turn_tile(0, 1, True)
            gram_tile(0, 1, True)

            def body(b, second):
                turn_tile(b, 0, False)
                pick(b, False)
                turn_gram(b - 1, second)
                gram_tile(b, 0, False)
                turn_pairs(b - 1)
                turn_tile(b, 1, False)
                layer1(b - 1, second)
                gram_tile(b, 1, False)
                layer2(b - 1)
                layer3(b - 1)

            body(1, True)
            with pe.Fori(2, NB) as b:
                body(b, False)
            turn_gram(NB - 1, False)
            turn_pairs(NB - 1)
            layer1(NB - 1, False)
            layer2(NB - 1)
            layer3(NB - 1)

        @block.scalar
        def _(act):
            def copy_tile(b, u, first):
                if not first:
                    act.wait_ge(gram_made, ((b - 1) * U + u + 1) * GB)
                    act.wait_ge(dense_t_made, b)
                for g, (lo, hi) in enumerate(GROUPS):
                    n = TURN_AT[u] + g
                    act.wait_ge(turned, b * TURNS + n + 1)
                    src = turn_bank[n % 2][:, 0:(hi - lo) * P].rearrange("d (f j) -> d j f", j=P)
                    nc.scalar.copy(slot_t[:, u, :, lo:hi], src).then_inc(turn_copied, 1)

            def copy_picked(b):
                if not isinstance(b, int) or b > 0:
                    act.wait_ge(gram_made, b * U * GB)
                for g, (lo, hi) in enumerate(OGROUPS):
                    n = OH_AT + g
                    act.wait_ge(turned, b * TURNS + n + 1)
                    dst = slot_t[:, :, :, NG + lo:NG + hi].rearrange("d u j f -> d (u j) f")
                    src = turn_bank[n % 2][:, 0:(hi - lo) * BS].rearrange("d (f j) -> d j f", j=BS)
                    nc.scalar.copy(dst, src).then_inc(turn_copied, 1)

            def copy_dense(b, first):
                act.wait_ge(turn_copied, b * TURNS + TURN_AT[1] + 1)
                if not first:
                    act.wait_ge(l1_made, b * (N1 // 2))
                src = slot_t[:, :, :, 0].rearrange("d u (s k) -> d s u k", s=S)
                dst = dense_t[:].rearrange("d (s u k) -> d s u k", s=S, u=U)
                nc.scalar.copy(dst, src).then_inc(dense_t_made, 1)

            def relu1(b):
                for n in range(N1):
                    if n % 2 == 0:
                        act.wait_ge(l1_made, b * (N1 // 2) + n // 2 + 1)
                    nc.scalar.activation(h1[:, n, :], mlp_bank[n // 2][:, (n % 2) * BS:(n % 2 + 1) * BS],
                                         ACT.Relu, bias=b1_sb[:, n:n + 1]).then_inc(h1_made, 1)

            def relu2(b):
                act.wait_ge(l2_made, b + 1)
                for m in range(N2):
                    nc.scalar.activation(h2[:, m, :], mlp_bank[0][:, m * BS:(m + 1) * BS],
                                         ACT.Relu, bias=b2_sb[:, m:m + 1]).then_inc(h2_made, 1)

            def store_y(b, first):
                act.wait_ge(l3_made, b + 1)
                if not first:
                    act.wait_ge(out_stored, b * 16)
                src = mlp_bank[1][0:1, 0:BS].rearrange("o (s u k) -> o s u k", s=S, u=U)
                dst = y_row[:].rearrange("o (u s k) -> o s u k", s=S, u=U)
                nc.scalar.copy(dst, src).then_inc(y_made, 1)
                act.wait_ge(y_made, b + 1)
                act.dma_start(out[bass.ds(b * BS, BS), :].rearrange("j o -> o j"), y_row[:]).then_inc(out_stored, 16)

            for i in range(NOH):
                act.wait_ge(tbl_landed[i % 2], (i // 2 + 1) * 16)
                nc.scalar.copy(tbl_hi[i][0:CR], tbl_raw[i % 2][0:CR]).then_inc(hi_made, 1)
            act.wait_ge(weights_landed, 7 * 16)
            copy_tile(0, 0, True)
            copy_picked(0)
            copy_tile(0, 1, True)
            copy_dense(0, True)

            def body(b, second):
                copy_tile(b, 0, False)
                copy_picked(b)
                copy_tile(b, 1, False)
                relu1(b - 1)
                copy_dense(b, False)
                relu2(b - 1)
                store_y(b - 1, second)

            body(1, True)
            with act.Fori(2, NB) as b:
                body(b, False)
            relu1(NB - 1)
            relu2(NB - 1)
            store_y(NB - 1, False)
            act.wait_ge(out_stored, NB * 16)

        @block.vector
        def _(dve):
            def make_onehot(b, i, first):
                if i == 0:
                    dve.wait_ge(ids_bc_landed, (b + 1) * 16)
                if i >= OH_BUFS:
                    dve.wait_ge(turned, b * TURNS + OH_AT + (i - OH_BUFS) // 2 + 1)
                elif not first:
                    last = [m for m in range(NOH) if m % OH_BUFS == i][-1]
                    dve.wait_ge(turned, (b - 1) * TURNS + OH_AT + last // 2 + 1)
                nc.vector.tensor_tensor(
                    onehot[i % OH_BUFS][0:CR], ids_bc[0:CR, i:i + 1, :].to_broadcast([CR, NCH, BS]),
                    row_of[0:CR, :].unsqueeze(2).to_broadcast([CR, NCH, BS]), ALU.is_equal,
                ).then_inc(onehot_made, 1)

            def copy_gram(b, u):
                for h in range(GB):
                    dve.wait_ge(gram_made, (b * U + u) * GB + h + 1)
                    src = gram_bank[h][:].rearrange("p (k c) -> p c k", c=PAD)[:, 0:F, :]
                    at = u * K + h * SETS
                    nc.vector.tensor_copy(gram[:, :, at:at + SETS], src).then_inc(gram_copied, 1)

            def pack_pairs(b):
                for n, (lo, hi) in enumerate(CGROUPS):
                    dve.wait_ge(post_made, b * POSTS + n + 1)
                    for c in range(lo, hi):
                        src = post_bank[n % 2][0:U * K, (c - lo) * P:(c - lo + 1) * P]
                        src = src.rearrange("p (s a) -> p s a", a=PAD)[:, :, c + 1:F + 1]
                        cp = nc.vector.tensor_copy(pairs[:, :, pair_at[c]:pair_at[c + 1]], src)
                    cp.then_inc(post_copied, 1)

            def copy_pairs_t(b):
                for i, (lo, hi) in enumerate(((0, 2), (2, 3))):
                    n = len(CGROUPS) + i
                    dve.wait_ge(post_made, b * POSTS + n + 1)
                    src = post_bank[n % 2][0:PC, 0:(hi - lo) * BS].rearrange("p (q j) -> p q j", j=BS)
                    nc.vector.tensor_copy(pairs_t[:, lo:hi, :], src).then_inc(post_copied, 1)

            nc.vector.memset(slot_t[:, :, :, F + 1:PAD], 0.0).then_inc(pads_made, 1)
            dve.wait_ge(consts_made, 2)
            for i in range(NOH):
                dve.wait_ge(hi_made, i + 1)
                nc.vector.tensor_tensor(tbl_lo[i][0:CR], tbl_raw[i % 2][0:CR],
                                        tbl_hi[i][0:CR].bitcast(F32), ALU.subtract).then_inc(lo_made, 1)
                if i < OH_BUFS:
                    make_onehot(0, i, True)
            dve.wait_ge(weights_landed, 7 * 16)
            nc.vector.tensor_tensor(w_dense[:], w_dense[:], w_dense2[:], ALU.add).then_inc(w_dense_made, 1)

            def rest(b, first):
                for i in range(OH_BUFS, NOH):
                    make_onehot(b, i, first)
                if not first:
                    pack_pairs(b - 1)
                copy_gram(b, 0)
                if not first:
                    copy_pairs_t(b - 1)
                copy_gram(b, 1)

            rest(0, True)
            for i in range(OH_BUFS):
                make_onehot(1, i, False)
            with dve.Fori(1, NB - 1) as b:
                rest(b, False)
                for i in range(OH_BUFS):
                    make_onehot(b + 1, i, False)
            rest(NB - 1, False)
            pack_pairs(NB - 1)
            copy_pairs_t(NB - 1)


def kernel(**inputs):
    import numpy as _np
    import concourse.bacc as _bacc
    from concourse import mybir as _mybir
    from concourse.bass_utils import run_bass_kernel_spmd as _run

    nc = _bacc.Bacc("TRN2", target_bir_lowering=False, num_devices=1)
    arrays = {}

    def given(name, array):
        a = _np.ascontiguousarray(array)
        arrays[f"in_{name}_dram"] = a
        return nc.dram_tensor(f"in_{name}_dram", a.shape, _mybir.dt.from_np(a.dtype), kind="ExternalInput").ap()

    dense = given("r_dense_features", inputs["r_dense_features"])
    ids = given("ids", inputs["ids"])
    ids_t = given("ids_t", _np.asarray(inputs["ids"]).T)
    tables = [given(f"tbl_{t}", inputs[f"tbl_{t}"]) for t in range(inputs["ids"].shape[1])]
    w1, w2 = given("W_top1", inputs["W_top1"]), given("W_top2", inputs["W_top2"])
    b1, b2, w3 = (given(n, _np.asarray(inputs[n]).reshape(-1, 128).T) for n in ("b_top1", "b_top2", "W_top3"))
    out = nc.dram_tensor("out_0_dram", (dense.shape[0], 1), _mybir.dt.float32, kind="ExternalOutput").ap()
    build_dlrm_tower(nc, dense, ids, ids_t, tables, w1, b1, w2, b2, w3, out)
    r = _run(nc, [arrays], core_ids=[0])
    return r.results[0]["out_0_dram"]
```

```python
from contextlib import ExitStack

import concourse.bass as bass
from concourse import mybir

ALU = mybir.AluOpType
ACT = mybir.ActivationFunctionType
F32 = mybir.dt.float32
F32R = mybir.dt.float32r
I32 = mybir.dt.int32

P = 128
U = 2
BS = U * P
NOH = 7
S = 4
K = P // S
PAD = 32
OH_BUFS = 3
TB = 3
BANK = 512


def last_use(n, per_block, buffers):
    if n >= buffers:
        return per_block + n - buffers + 1
    before = [m for m in range(per_block) if m % buffers == n % buffers]
    return before[-1] + 1


def build_dlrm_tower(nc, dense, ids, ids_t, tables, w1, b1, w2, b2, w3, out):
    B, D = dense.shape
    F = len(tables)
    TG = F - NOH
    NB = B // BS
    VOH = tables[TG].shape[0]
    NCH = 8
    CR = VOH // NCH
    NG = TG + 1
    GROUPS = [(g, min(g + 4, NG)) for g in range(0, NG, 4)]
    OGROUPS = [(g, min(g + 2, NOH)) for g in range(0, NOH, 2)]
    NGR, NOG = len(GROUPS), len(OGROUPS)
    TILE_GROUPS = U * NGR
    TURNS = TILE_GROUPS + NOG
    TURN_ORDER = [(0, 0), (0, 1), ("oh", 0)] + [(0, g) for g in range(2, NGR)]
    TURN_ORDER += [("oh", g) for g in range(1, NOG)] + [(1, g) for g in range(NGR)]
    turn_use = {what: n for n, what in enumerate(TURN_ORDER)}
    TURNED_0 = NGR + NOG
    NPAIR = (F + 1) * F // 2
    PC = NPAIR // 3
    H1, H2 = w1.shape[1], w2.shape[1]
    N1, N2 = H1 // P, H2 // P
    SETS = BANK // PAD
    GB = K // SETS
    CPB = 4
    CGROUPS = [(c, min(c + CPB, F)) for c in range(0, F, CPB)]
    POSTS = len(CGROUPS) + 2
    assert D == P and NB * BS == B and CR * NCH == VOH and CR <= P and PC * 3 == NPAIR and PC <= P
    assert all(t.shape[0] == VOH for t in tables[TG:])
    pair_at = [c * F - c * (c - 1) // 2 for c in range(F + 1)]

    with ExitStack() as ctx:
        def sb(name, shape, dt=F32):
            return ctx.enter_context(nc.sbuf_tensor(name, shape, dt))

        def psum(name):
            return ctx.enter_context(nc.psum_tensor(name, [P, BANK], F32))

        def sem(name):
            return ctx.enter_context(nc.semaphore(name))

        ones = sb("ones", [P, P])
        ident = sb("ident", [P, P])
        row_of = sb("row_of", [P, NCH], I32)
        idx = [sb(f"idx{u}", [P, F], I32) for u in range(U)]
        rows = [sb(f"rows{u}", [P, NG, D]) for u in range(U)]
        ids_bc = sb("ids_bc", [P, NOH, BS], I32)
        onehot = [sb(f"onehot{i}", [P, NCH, BS], F32R) for i in range(OH_BUFS)]
        raw = [sb(f"raw{i}", [P, 3 * H1]) for i in range(2)]
        tbl_raw = [raw[i][:, 0:NCH * D].rearrange("p (c d) -> p c d", c=NCH) for i in range(2)]
        w_dense = raw[0][:, 0:H1]
        w_dense2 = raw[0][:, H1:2 * H1]
        w_pair = raw[1][0:PC, :].rearrange("p (q n) -> p q n", q=3)
        w2_raw = raw[0][:, 0:N1 * H2].rearrange("p (k n) -> p k n", k=N1)
        tbl_hi = [sb(f"tbl_hi{i}", [P, NCH, D], F32R) for i in range(NOH)]
        tbl_lo = [sb(f"tbl_lo{i}", [P, NCH, D], F32R) for i in range(NOH)]
        slot_flat = sb("slot_flat", [P, U, P * (F + 1) + PAD - F - 1])
        slot_t = slot_flat[:, :, 0:P * (F + 1)].rearrange("d u (j f) -> d u j f", f=F + 1)
        gram = sb("gram", [P, F, U * K])
        pairs = sb("pairs", [U * K, S, NPAIR])
        pairs_hi = sb("pairs_hi", [PC, 3, BS], F32R)
        pairs_lo = sb("pairs_lo", [PC, 3, BS], F32R)
        dense_hi = sb("dense_hi", [P, BS], F32R)
        dense_lo = sb("dense_lo", [P, BS], F32R)
        h1 = sb("h1", [P, N1, BS])
        h1_hi = sb("h1_hi", [P, N1, BS], F32R)
        h1_lo = sb("h1_lo", [P, N1, BS], F32R)
        h2 = sb("h2", [P, N2, BS])
        y_row = sb("y_row", [1, BS])
        w_dense_hi = sb("w_dense_hi", [P, H1], F32R)
        w_dense_lo = sb("w_dense_lo", [P, H1], F32R)
        w_pair_hi = sb("w_pair_hi", [PC, 3, H1], F32R)
        w_pair_lo = sb("w_pair_lo", [PC, 3, H1], F32R)
        w2_hi = sb("w2_hi", [P, N1, H2], F32R)
        w2_lo = sb("w2_lo", [P, N1, H2], F32R)
        w3_sb = sb("w3_sb", [P, N2])
        b1_sb = sb("b1_sb", [P, N1])
        b2_sb = sb("b2_sb", [P, N2])

        turn_bank = [psum(f"turn_bank{i}") for i in range(TB)]
        gram_bank = psum("gram_bank")
        post_bank = [psum(f"post_bank{i}") for i in range(2)]
        mlp_bank = [psum(f"mlp_bank{i}") for i in range(2)]

        idx_landed = [sem(f"idx_landed{u}") for u in range(U)]
        dense_landed = [sem(f"dense_landed{u}") for u in range(U)]
        rows_landed = [[sem(f"rows_landed{u}_{g}") for g in range(NGR)] for u in range(U)]
        ids_bc_landed = sem("ids_bc_landed")
        tbl_landed = [sem(f"tbl_landed{i}") for i in range(2)]
        w1_landed = sem("w1_landed")
        w2_landed = sem("w2_landed")
        vectors_landed = sem("vectors_landed")
        out_stored = sem("out_stored")
        ones_made = sem("ones_made")
        consts_made = sem("consts_made")
        pads_made = sem("pads_made")
        w_dense_made = sem("w_dense_made")
        w_hi_made = sem("w_hi_made")
        w_lo_made = sem("w_lo_made")
        hi_made = sem("hi_made")
        lo_made = sem("lo_made")
        onehot_made = sem("onehot_made")
        turned = sem("turned")
        picked = sem("picked")
        turn_copied = sem("turn_copied")
        dense_hi_made = sem("dense_hi_made")
        dense_lo_made = sem("dense_lo_made")
        gram_made = sem("gram_made")
        gram_copied = sem("gram_copied")
        post_made = sem("post_made")
        post_copied = sem("post_copied")
        pairs_hi_made = sem("pairs_hi_made")
        l1_made = sem("l1_made")
        h1_made = sem("h1_made")
        h1_lo_made = sem("h1_lo_made")
        l2_made = sem("l2_made")
        h2_made = sem("h2_made")
        l3_made = sem("l3_made")
        y_made = sem("y_made")
        sp_passed = sem("sp_passed")
        pool_passed = sem("pool_passed")
        pe_passed = sem("pe_passed")

        block = ctx.enter_context(nc.Block())

        @block.sync
        def _(sp):
            def load_idx(b, u):
                sp.dma_start(idx[u][:], ids[bass.ds(b * BS + u * P, P), :]).then_inc(idx_landed[u], 16)

            def load_dense(b, u):
                sp.dma_start(rows[u][:, 0, :],
                             dense[bass.ds(b * BS + u * P, P), :]).then_inc(dense_landed[u], 16)

            def load_ids_bc(b):
                src = ids_t[TG:F, bass.ds(b * BS, BS)].partition_broadcast(P)
                sp.dma_start(ids_bc[:], src).then_inc(ids_bc_landed, 16)

            load_idx(0, 0)
            load_dense(0, 0)
            load_idx(0, 1)
            load_ids_bc(0)
            for i in range(NOH):
                if i >= 2:
                    sp.wait_ge(lo_made, i - 1)
                src = tables[TG + i].rearrange("(c p) d -> p c d", p=CR)
                sp.dma_start(tbl_raw[i % 2][0:CR], src).then_inc(tbl_landed[i % 2], 16)
            load_dense(0, 1)
            sp.dma_start(w3_sb[:], w3).then_inc(vectors_landed, 16)
            sp.dma_start(b1_sb[:], b1).then_inc(vectors_landed, 16)
            sp.dma_start(b2_sb[:], b2).then_inc(vectors_landed, 16)
            with sp.Fori(1, NB) as b:
                for u in range(U):
                    for g in range(NGR):
                        lo, hi = GROUPS[g]
                        sp.wait_ge(rows_landed[u][g], b * 16 * (hi - max(lo, 1)))
                        sp.sem_inc(sp_passed, 1)
                    load_idx(b, u)
                    sp.wait_ge(turned, (b - 1) * TILE_GROUPS + u * NGR + 1)
                    load_dense(b, u)
                    if u == 0:
                        sp.wait_ge(onehot_made, b * NOH)
                        load_ids_bc(b)

        @block.gpsimd
        def _(pool):
            nc.gpsimd.memset(ones[:], 1.0).then_inc(ones_made, 1)
            pool.wait_ge(ones_made, 1)
            nc.gpsimd.affine_select(out=ident[:], in_=ones[:], compare_op=ALU.is_equal, fill=0.0, base=0,
                                    pattern=[[-1, P]], channel_multiplier=1).then_inc(consts_made, 1)
            nc.gpsimd.iota(row_of[:], pattern=[[CR, NCH]], base=0, channel_multiplier=1).then_inc(consts_made, 1)

            def gather(b, first):
                for u in range(U):
                    pool.wait_ge(idx_landed[u], (b + 1) * 16)
                    for g, (lo, hi) in enumerate(GROUPS):
                        if not first:
                            pool.wait_ge(turned, (b - 1) * TILE_GROUPS + u * NGR + g + 1)
                            pool.sem_inc(pool_passed, 1)
                        for slot in range(max(lo, 1), hi):
                            t = slot - 1
                            nc.gpsimd.indirect_dma_start(
                                rows[u][:, slot, :], None, tables[t],
                                bass.IndirectOffsetOnAxis(ap=idx[u][:, t:t + 1], axis=0),
                            ).then_inc(rows_landed[u][g], 16)

            gather(0, True)
            with pool.Fori(1, NB) as b:
                gather(b, False)

        @block.tensor
        def _(pe):
            def turn_tile(b, u, first, groups=range(NGR)):
                for g in groups:
                    lo, hi = GROUPS[g]
                    n = turn_use[u, g]
                    if lo == 0:
                        pe.wait_ge(dense_landed[u], (b + 1) * 16)
                    pe.wait_ge(rows_landed[u][g], (b + 1) * 16 * (hi - max(lo, 1)))
                    if not first or n >= TB:
                        pe.wait_ge(turn_copied, (b - 1) * TURNS + last_use(n, TURNS, TB))
                    for slot in range(lo, hi):
                        j = slot - lo
                        mm = nc.tensor.transpose(turn_bank[n % TB][:, j * P:(j + 1) * P],
                                                 rows[u][:, slot, :], ident[:])
                    mm.then_inc(turned, 1)

            def pick(b, first, groups=range(NOG)):
                for g in groups:
                    lo, hi = OGROUPS[g]
                    n = turn_use["oh", g]
                    if not first or n >= TB:
                        pe.wait_ge(turn_copied, (b - 1) * TURNS + last_use(n, TURNS, TB))
                    for i in range(lo, hi):
                        pe.wait_ge(onehot_made, b * NOH + i + 1)
                        if first:
                            pe.wait_ge(lo_made, i + 1)
                        for c in range(NCH):
                            for part in (tbl_hi, tbl_lo):
                                mm = nc.tensor.matmul(
                                    turn_bank[n % TB][:, (i - lo) * BS:(i - lo + 1) * BS],
                                    part[i][0:CR, c, :], onehot[i % OH_BUFS][0:CR, c, :],
                                    start=(c == 0 and part is tbl_hi), stop=(c == NCH - 1 and part is tbl_lo))
                        mm.then_inc(picked, 1)

            def gram_tile(b, u, first, banks=range(GB)):
                pe.wait_ge(turn_copied, b * TURNS + (TURNS if u else TURNED_0))
                for h in banks:
                    if not first or u or h:
                        pe.wait_ge(gram_copied, (b * U + u) * GB + h)
                    for k in range(SETS):
                        for s in range(S):
                            at = s * K + h * SETS + k
                            mm = nc.tensor.matmul(gram_bank[s * PAD:(s + 1) * PAD, k * PAD:k * PAD + F],
                                                  slot_flat[:, u, at * (F + 1):at * (F + 1) + PAD],
                                                  slot_t[:, u, at, 0:F],
                                                  start=True, stop=True, tile_position=(0, s * PAD))
                    mm.then_inc(gram_made, 1)

            def turn_gram(b, first, groups=range(len(CGROUPS))):
                for n in groups:
                    lo, hi = CGROUPS[n]
                    if n == 0:
                        pe.wait_ge(gram_copied, (b + 1) * U * GB)
                    if not first or n >= 2:
                        pe.wait_ge(post_copied, (b - 1) * POSTS + last_use(n, POSTS, 2))
                        pe.sem_inc(pe_passed, 1)
                    for c in range(lo, hi):
                        mm = nc.tensor.transpose(post_bank[n % 2][0:U * K, (c - lo) * P:(c - lo + 1) * P],
                                                 gram[:, c, :], ident[:])
                    mm.then_inc(post_made, 1)

            def turn_pairs(b):
                pe.wait_ge(post_copied, b * POSTS + len(CGROUPS))
                pe.sem_inc(pe_passed, 1)
                for i, chunks in enumerate(((0, 1), (2,))):
                    n = len(CGROUPS) + i
                    for j, q in enumerate(chunks):
                        for s in range(S):
                            at = j * BS + s * U * K
                            mm = nc.tensor.transpose(post_bank[n % 2][0:PC, at:at + U * K],
                                                     pairs[:, s, q * PC:(q + 1) * PC], ident[0:U * K, 0:U * K])
                    mm.then_inc(post_made, 1)

            def split_product(dst, w_hi, w_lo, x_hi, x_lo, start, stop):
                nc.tensor.matmul(dst, w_hi, x_hi, start=start, stop=False)
                nc.tensor.matmul(dst, w_hi, x_lo, start=False, stop=False)
                return nc.tensor.matmul(dst, w_lo, x_hi, start=False, stop=stop)

            def layer1(b, first):
                if first:
                    pe.wait_ge(w_lo_made, 3)
                    pe.wait_ge(vectors_landed, 3 * 16)
                pe.wait_ge(dense_lo_made, b + 1)
                pe.wait_ge(post_copied, (b + 1) * POSTS)
                for n in range(N1):
                    if not first and n == 0:
                        pe.wait_ge(h2_made, b * N2)
                    if not first and n == 2:
                        pe.wait_ge(y_made, b)
                    dst = mlp_bank[n // 2][:, (n % 2) * BS:(n % 2 + 1) * BS]
                    at = slice(n * P, (n + 1) * P)
                    split_product(dst, w_dense_hi[:, at], w_dense_lo[:, at], dense_hi[:], dense_lo[:], True, False)
                    for q in range(3):
                        mm = split_product(dst, w_pair_hi[:, q, at], w_pair_lo[:, q, at],
                                           pairs_hi[:, q, :], pairs_lo[:, q, :], False, q == 2)
                    if n % 2:
                        mm.then_inc(l1_made, 1)

            def layer2(b, parts=range(N2)):
                for m in parts:
                    for k in range(N1):
                        if m == 0:
                            pe.wait_ge(h1_lo_made, b * N1 + max(k, 1) + 1)
                        at = slice(m * P, (m + 1) * P)
                        mm = split_product(mlp_bank[0][:, m * BS:(m + 1) * BS], w2_hi[:, k, at], w2_lo[:, k, at],
                                           h1_hi[:, k, :], h1_lo[:, k, :], k == 0, k == N1 - 1)
                if m == N2 - 1:
                    mm.then_inc(l2_made, 1)

            def layer3(b):
                for k in range(N2):
                    pe.wait_ge(h2_made, b * N2 + k + 1)
                    mm = nc.tensor.matmul(mlp_bank[1][0:1, 0:BS], w3_sb[:, k:k + 1], h2[:, k, :],
                                          start=(k == 0), stop=(k == N2 - 1))
                mm.then_inc(l3_made, 1)

            pe.wait_ge(consts_made, 1)
            turn_tile(0, 0, True, range(0, 2))
            pick(0, True, range(0, 1))
            turn_tile(0, 0, True, range(2, NGR))
            pick(0, True, range(1, NOG))
            pe.wait_ge(pads_made, 1)
            gram_tile(0, 0, True)
            turn_tile(0, 1, True)
            gram_tile(0, 1, True, range(0, 1))

            def body(b, second):
                turn_tile(b, 0, False, range(0, 2))
                pick(b, False, range(0, 1))
                gram_tile(b - 1, 1, second, range(1, GB))
                turn_tile(b, 0, False, range(2, NGR))
                turn_gram(b - 1, second, range(0, 5))
                pick(b, False, range(1, 2))
                turn_gram(b - 1, second, range(5, len(CGROUPS)))
                pick(b, False, range(2, NOG))
                turn_pairs(b - 1)
                gram_tile(b, 0, False, range(0, 1))
                layer1(b - 1, second)
                gram_tile(b, 0, False, range(1, GB))
                turn_tile(b, 1, False, range(0, 2))
                layer2(b - 1, range(0, 1))
                turn_tile(b, 1, False, range(2, 3))
                layer2(b - 1, range(1, N2))
                turn_tile(b, 1, False, range(3, NGR))
                layer3(b - 1)
                gram_tile(b, 1, False, range(0, 1))

            body(1, True)
            with pe.Fori(2, NB) as b:
                body(b, False)
            gram_tile(NB - 1, 1, False, range(1, GB))
            turn_gram(NB - 1, False)
            turn_pairs(NB - 1)
            layer1(NB - 1, False)
            layer2(NB - 1)
            layer3(NB - 1)

        @block.scalar
        def _(act):
            def copy_tile(b, u, first, groups=range(NGR)):
                if not first and 0 in groups:
                    act.wait_ge(gram_made, ((b - 1) * U + u + 1) * GB)
                    act.wait_ge(dense_lo_made, b)
                for g in groups:
                    lo, hi = GROUPS[g]
                    n = turn_use[u, g]
                    act.wait_ge(turned, b * TILE_GROUPS + u * NGR + g + 1)
                    src = turn_bank[n % TB][:, 0:(hi - lo) * P].rearrange("d (f j) -> d j f", j=P)
                    nc.scalar.copy(slot_t[:, u, :, lo:hi], src).then_inc(turn_copied, 1)

            def copy_picked(b, first, groups):
                if not first and 0 in groups:
                    act.wait_ge(gram_made, b * U * GB)
                for g in groups:
                    lo, hi = OGROUPS[g]
                    n = turn_use["oh", g]
                    act.wait_ge(picked, b * NOH + hi)
                    dst = slot_t[:, :, :, NG + lo:NG + hi]
                    src = turn_bank[n % TB][:, 0:(hi - lo) * BS].rearrange("d (f u j) -> d u j f", u=U, j=P)
                    nc.scalar.copy(dst, src).then_inc(turn_copied, 1)

            def copy_dense(b, first):
                act.wait_ge(turn_copied, b * TURNS + turn_use[1, 0] + 1)
                if not first:
                    act.wait_ge(l1_made, b * (N1 // 2))
                src = slot_t[:, :, :, 0].rearrange("d u (s k) -> d s u k", s=S)
                dst = dense_hi[:].rearrange("d (s u k) -> d s u k", s=S, u=U)
                nc.scalar.copy(dst, src).then_inc(dense_hi_made, 1)

            def relu1(b):
                for n in range(N1):
                    if n % 2 == 0:
                        act.wait_ge(l1_made, b * (N1 // 2) + n // 2 + 1)
                    src = mlp_bank[n // 2][:, (n % 2) * BS:(n % 2 + 1) * BS]
                    nc.scalar.activation(h1[:, n, :], src, ACT.Relu, bias=b1_sb[:, n:n + 1])
                    nc.scalar.activation(h1_hi[:, n, :], src, ACT.Relu, bias=b1_sb[:, n:n + 1]).then_inc(h1_made, 1)

            def relu2(b):
                act.wait_ge(l2_made, b + 1)
                for m in range(N2):
                    nc.scalar.activation(h2[:, m, :], mlp_bank[0][:, m * BS:(m + 1) * BS],
                                         ACT.Relu, bias=b2_sb[:, m:m + 1]).then_inc(h2_made, 1)

            def store_y(b, first):
                act.wait_ge(l3_made, b + 1)
                if not first:
                    act.wait_ge(out_stored, b * 16)
                src = mlp_bank[1][0:1, 0:BS].rearrange("o (s u k) -> o s u k", s=S, u=U)
                dst = y_row[:].rearrange("o (u s k) -> o s u k", s=S, u=U)
                nc.scalar.copy(dst, src).then_inc(y_made, 1)
                act.wait_ge(y_made, b + 1)
                act.dma_start(out[bass.ds(b * BS, BS), :].rearrange("j o -> o j"), y_row[:]).then_inc(out_stored, 16)

            for i in range(NOH):
                act.wait_ge(tbl_landed[i % 2], (i // 2 + 1) * 16)
                nc.scalar.copy(tbl_hi[i][0:CR], tbl_raw[i % 2][0:CR]).then_inc(hi_made, 1)
                if i == 2:
                    copy_tile(0, 0, True, range(0, 2))
                if i == 4:
                    copy_picked(0, True, range(0, 1))
            copy_tile(0, 0, True, range(2, NGR))
            copy_picked(0, True, range(1, NOG))
            act.wait_ge(lo_made, NOH)
            act.dma_start(w_dense, w1[0:D, :]).then_inc(w1_landed, 16)
            act.dma_start(w_dense2, w1[D + NPAIR:2 * D + NPAIR, :]).then_inc(w1_landed, 16)
            act.dma_start(w_pair, w1[D:D + NPAIR, :].rearrange("(c p) n -> p c n", p=PC)).then_inc(w1_landed, 16)
            copy_tile(0, 1, True, range(0, 2))
            act.wait_ge(w_dense_made, 1)
            nc.scalar.copy(w_dense_hi[:], w_dense).then_inc(w_hi_made, 1)
            nc.scalar.copy(w_pair_hi[:], w_pair).then_inc(w_hi_made, 1)
            act.wait_ge(w_lo_made, 1)
            act.dma_start(w2_raw, w2.rearrange("(k p) n -> p k n", p=P)).then_inc(w2_landed, 16)
            copy_tile(0, 1, True, range(2, NGR))
            copy_dense(0, True)
            act.wait_ge(w2_landed, 16)
            nc.scalar.copy(w2_hi[:], w2_raw).then_inc(w_hi_made, 1)

            def body(b, second):
                copy_tile(b, 0, False, range(0, 2))
                copy_picked(b, False, range(0, 1))
                copy_tile(b, 0, False, range(2, NGR))
                copy_picked(b, False, range(1, NOG))
                relu1(b - 1)
                copy_tile(b, 1, False, range(0, 3))
                relu2(b - 1)
                copy_tile(b, 1, False, range(3, NGR))
                store_y(b - 1, second)
                copy_dense(b, False)

            body(1, True)
            with act.Fori(2, NB) as b:
                body(b, False)
            relu1(NB - 1)
            relu2(NB - 1)
            store_y(NB - 1, False)
            act.wait_ge(out_stored, NB * 16)

        @block.vector
        def _(dve):
            def make_onehot(b, i, first):
                if i == 0:
                    dve.wait_ge(ids_bc_landed, (b + 1) * 16)
                if not first or i >= OH_BUFS:
                    dve.wait_ge(picked, (b - 1) * NOH + last_use(i, NOH, OH_BUFS))
                nc.vector.tensor_tensor(
                    onehot[i % OH_BUFS][0:CR], ids_bc[0:CR, i:i + 1, :].to_broadcast([CR, NCH, BS]),
                    row_of[0:CR, :].unsqueeze(2).to_broadcast([CR, NCH, BS]), ALU.is_equal,
                ).then_inc(onehot_made, 1)

            def copy_gram(b, u, h):
                dve.wait_ge(gram_made, (b * U + u) * GB + h + 1)
                src = gram_bank[:].rearrange("p (k c) -> p c k", c=PAD)[:, 0:F, :]
                at = u * K + h * SETS
                nc.vector.tensor_copy(gram[:, :, at:at + SETS], src).then_inc(gram_copied, 1)

            def pack_pairs(b, groups=range(len(CGROUPS))):
                for n in groups:
                    lo, hi = CGROUPS[n]
                    dve.wait_ge(post_made, b * POSTS + n + 1)
                    for c in range(lo, hi):
                        src = post_bank[n % 2][0:U * K, (c - lo) * P:(c - lo + 1) * P]
                        src = src.rearrange("p (s a) -> p s a", a=PAD)[:, :, c + 1:F + 1]
                        cp = nc.vector.tensor_copy(pairs[:, :, pair_at[c]:pair_at[c + 1]], src)
                    cp.then_inc(post_copied, 1)

            def split_pairs(b):
                for i, (lo, hi) in enumerate(((0, 2), (2, 3))):
                    n = len(CGROUPS) + i
                    dve.wait_ge(post_made, b * POSTS + n + 1)
                    src = post_bank[n % 2][0:PC, 0:(hi - lo) * BS].rearrange("p (q j) -> p q j", j=BS)
                    nc.vector.tensor_copy(pairs_hi[:, lo:hi, :], src).then_inc(pairs_hi_made, 1)
                    dve.wait_ge(pairs_hi_made, b * 2 + i + 1)
                    nc.vector.tensor_tensor(pairs_lo[:, lo:hi, :], src, pairs_hi[:, lo:hi, :].bitcast(F32),
                                            ALU.subtract).then_inc(post_copied, 1)

            def split_dense(b):
                dve.wait_ge(dense_hi_made, b + 1)
                nc.vector.tensor_tensor(
                    dense_lo[:].rearrange("d (s u k) -> d s u k", s=S, u=U),
                    slot_t[:, :, :, 0].rearrange("d u (s k) -> d s u k", s=S),
                    dense_hi[:].bitcast(F32).rearrange("d (s u k) -> d s u k", s=S, u=U),
                    ALU.subtract).then_inc(dense_lo_made, 1)

            def split_h1(b):
                for n in range(N1):
                    dve.wait_ge(h1_made, b * N1 + n + 1)
                    nc.vector.tensor_tensor(h1_lo[:, n, :], h1[:, n, :], h1_hi[:, n, :].bitcast(F32),
                                            ALU.subtract).then_inc(h1_lo_made, 1)

            nc.vector.memset(slot_flat[:, :, P * (F + 1):], 0.0).then_inc(pads_made, 1)
            dve.wait_ge(consts_made, 2)
            for i in range(NOH):
                dve.wait_ge(hi_made, i + 1)
                nc.vector.tensor_tensor(tbl_lo[i][0:CR], tbl_raw[i % 2][0:CR],
                                        tbl_hi[i][0:CR].bitcast(F32), ALU.subtract).then_inc(lo_made, 1)
                if i < OH_BUFS:
                    make_onehot(0, i, True)
            for i in range(OH_BUFS, NOH):
                make_onehot(0, i, True)

            def split_weight(i, lo, hi, whole):
                dve.wait_ge(w_hi_made, i + 1)
                nc.vector.tensor_tensor(lo[:], whole, hi[:].bitcast(F32), ALU.subtract).then_inc(w_lo_made, 1)

            copy_gram(0, 0, 0)
            dve.wait_ge(w1_landed, 3 * 16)
            nc.vector.tensor_tensor(w_dense, w_dense, w_dense2, ALU.add).then_inc(w_dense_made, 1)
            copy_gram(0, 0, 1)
            split_weight(0, w_dense_lo, w_dense_hi, w_dense)
            split_weight(1, w_pair_lo, w_pair_hi, w_pair)
            for i in range(OH_BUFS):
                make_onehot(1, i, False)
            split_dense(0)
            copy_gram(0, 1, 0)
            split_weight(2, w2_lo, w2_hi, w2_raw)

            def steps(b, last):
                make_onehot(b, OH_BUFS, False)
                copy_gram(b - 1, 1, 1)
                pack_pairs(b - 1, range(0, 4))
                make_onehot(b, OH_BUFS + 1, False)
                pack_pairs(b - 1, range(4, 5))
                for i in range(OH_BUFS + 2, min(OH_BUFS + 3, NOH)):
                    make_onehot(b, i, False)
                pack_pairs(b - 1, range(5, len(CGROUPS)))
                for i in range(OH_BUFS + 3, NOH):
                    make_onehot(b, i, False)
                split_pairs(b - 1)
                copy_gram(b, 0, 0)
                split_h1(b - 1)
                copy_gram(b, 0, 1)
                if not last:
                    for i in range(OH_BUFS):
                        make_onehot(b + 1, i, False)
                split_dense(b)
                copy_gram(b, 1, 0)

            with dve.Fori(1, NB - 1) as b:
                steps(b, False)
            steps(NB - 1, True)
            copy_gram(NB - 1, 1, 1)
            pack_pairs(NB - 1)
            split_pairs(NB - 1)
            split_h1(NB - 1)


def kernel(**inputs):
    import numpy as _np
    import concourse.bacc as _bacc
    from concourse import mybir as _mybir
    from concourse.bass_utils import run_bass_kernel_spmd as _run

    nc = _bacc.Bacc("TRN2", target_bir_lowering=False, num_devices=1)
    arrays = {}

    def given(name, array):
        a = _np.ascontiguousarray(array)
        arrays[f"in_{name}_dram"] = a
        return nc.dram_tensor(f"in_{name}_dram", a.shape, _mybir.dt.from_np(a.dtype), kind="ExternalInput").ap()

    dense = given("r_dense_features", inputs["r_dense_features"])
    ids = given("ids", inputs["ids"])
    ids_t = given("ids_t", _np.asarray(inputs["ids"]).T)
    tables = [given(f"tbl_{t}", inputs[f"tbl_{t}"]) for t in range(inputs["ids"].shape[1])]
    w1, w2 = given("W_top1", inputs["W_top1"]), given("W_top2", inputs["W_top2"])
    b1, b2, w3 = (given(n, _np.asarray(inputs[n]).reshape(-1, 128).T) for n in ("b_top1", "b_top2", "W_top3"))
    out = nc.dram_tensor("out_0_dram", (dense.shape[0], 1), _mybir.dt.float32, kind="ExternalOutput").ap()
    build_dlrm_tower(nc, dense, ids, ids_t, tables, w1, b1, w2, b2, w3, out)
    r = _run(nc, [arrays], core_ids=[0])
    return r.results[0]["out_0_dram"]
```

```python
from contextlib import ExitStack

import concourse.bass as bass
from concourse import mybir

ALU = mybir.AluOpType
ACT = mybir.ActivationFunctionType
F32 = mybir.dt.float32
F32R = mybir.dt.float32r
I32 = mybir.dt.int32

P = 128
U = 2
BS = U * P
NOH = 8
S = 4
K = P // S
PAD = 32
OH_BUFS = 3
RAWS = 3
TB = 3
BANK = 512


def last_use(n, per_block, buffers):
    if n >= buffers:
        return per_block + n - buffers + 1
    before = [m for m in range(per_block) if m % buffers == n % buffers]
    return before[-1] + 1


def build_dlrm_tower(nc, dense, ids, ids_t, tables, w1, b1, w2, b2, w3, out):
    B, D = dense.shape
    F = len(tables)
    TG = F - NOH
    NB = B // BS
    VOH = tables[TG].shape[0]
    NCH = 8
    CR = VOH // NCH
    NG = TG + 1
    GROUPS = [(g, min(g + 4, NG)) for g in range(0, NG, 4)]
    OGROUPS = [(g, min(g + 2, NOH)) for g in range(0, NOH, 2)]
    NGR, NOG = len(GROUPS), len(OGROUPS)
    TILE_GROUPS = U * NGR
    TURNS = TILE_GROUPS + NOG
    TURN_ORDER = [(0, 0), ("oh", 0), (0, 1), (0, 2), ("oh", 1), ("oh", 2)] + [(0, g) for g in range(3, NGR - 1)]
    TURN_ORDER += [("oh", g) for g in range(3, NOG)] + [(0, NGR - 1)] + [(1, g) for g in range(NGR)]
    turn_use = {what: n for n, what in enumerate(TURN_ORDER)}
    TURNED_0 = NGR + NOG
    NPAIR = (F + 1) * F // 2
    pair_at = [c * F - c * (c - 1) // 2 for c in range(F + 1)]
    CS = next(c for c in range(F) if NPAIR - pair_at[c] <= P)
    FA, FB = pair_at[CS], NPAIR - pair_at[CS]
    CHUNKS = [(0, FB), (FA, NPAIR), (FB, FA)]
    H1, H2 = w1.shape[1], w2.shape[1]
    N1 = H1 // P
    SETS = BANK // PAD
    GB = K // SETS
    JGROUPS = [(j, min(j + 4, F - CS)) for j in range(0, F - CS, 4)]
    POSTS = len(JGROUPS) + 2
    assert NOH >= OH_BUFS + 4 and NGR >= 5
    assert D == P and NB * BS == B and CR * NCH == VOH and CR <= P and CS <= F - CS and FA - FB <= FB
    assert N1 * BS == NCH * D == 2 * H1 and U * H2 == H1 and S * FA <= N1 * H2
    assert all(t.shape[0] == VOH for t in tables[TG:])

    with ExitStack() as ctx:
        def sb(name, shape, dt=F32):
            return ctx.enter_context(nc.sbuf_tensor(name, shape, dt))

        def psum(name):
            return ctx.enter_context(nc.psum_tensor(name, [P, BANK], F32))

        def sem(name):
            return ctx.enter_context(nc.semaphore(name))

        ones = sb("ones", [P, P])
        ident = sb("ident", [P, P])
        row_of = sb("row_of", [P, NCH], I32)
        idx = [sb(f"idx{u}", [P, F], I32) for u in range(U)]
        rows = [sb(f"rows{u}", [P, NG, D]) for u in range(U)]
        ids_bc = sb("ids_bc", [P, NOH, BS], I32)
        onehot = [sb(f"onehot{i}", [P, NCH, BS], F32R) for i in range(OH_BUFS)]
        raw = [sb(f"raw{i}", [P, N1 * BS]) for i in range(2)]
        h1 = raw[0][:].rearrange("p (n j) -> p n j", j=BS)
        gram_flat = sb("gram", [P, (F - CS) * P])
        gram = gram_flat[:].rearrange("p (j c i) -> p j c i", c=2, i=U * K)
        tbl_raw = [x[:, 0:NCH * D].rearrange("p (c d) -> p c d", d=D) for x in (raw[0], raw[1], gram_flat)]
        w_dense, w_dense2 = raw[0][:, 0:H1], raw[0][:, H1:2 * H1]
        w_pair_01 = raw[1][0:FB, :].rearrange("p (q n) -> p q n", n=H1)
        h2 = sb("h2", [P, U, H2])
        pairs_flat = sb("pairs", [P, N1 * H2])
        pairs = pairs_flat[:, 0:S * FA].rearrange("p (s n) -> p s n", s=S)
        w2_raw = pairs_flat[:].rearrange("p (k n) -> p k n", n=H2)
        w_pair_2 = h2[0:FA - FB, :, :].rearrange("p u n -> p (u n)")
        tbl_hi = [sb(f"tbl_hi{i}", [P, NCH, D], F32R) for i in range(NOH)]
        tbl_lo = [sb(f"tbl_lo{i}", [P, NCH, D], F32R) for i in range(NOH)]
        slot_flat = sb("slot_flat", [P, U, P * (F + 1) + PAD - F - 1])
        slot_t = slot_flat[:, :, 0:P * (F + 1)].rearrange("d u (j f) -> d u j f", f=F + 1)
        pairs_hi = sb("pairs_hi", [FB, 3, BS], F32R)
        pairs_lo = sb("pairs_lo", [FB, 3, BS], F32R)
        dense_hi = sb("dense_hi", [P, BS], F32R)
        dense_lo = sb("dense_lo", [P, BS], F32R)
        h1_hi = sb("h1_hi", [P, N1, BS], F32R)
        h1_lo = sb("h1_lo", [P, N1, BS], F32R)
        y_cols = sb("y_cols", [P, NB * U])
        y_rows = sb("y_rows", [NB * U, P])
        w_dense_hi = sb("w_dense_hi", [P, H1], F32R)
        w_dense_lo = sb("w_dense_lo", [P, H1], F32R)
        w_pair_hi = sb("w_pair_hi", [FB, 3, H1], F32R)
        w_pair_lo = sb("w_pair_lo", [FB, 3, H1], F32R)
        w2_hi = sb("w2_hi", [P, N1, H2], F32R)
        w2_lo = sb("w2_lo", [P, N1, H2], F32R)
        b1_sb = sb("b1_sb", [P, N1])
        b2_bc = sb("b2_bc", [P, H2])
        w3_bc = sb("w3_bc", [P, H2])

        turn_bank = [psum(f"turn_bank{i}") for i in range(TB)]
        gram_bank = psum("gram_bank")
        post_bank = [psum(f"post_bank{i}") for i in range(2)]
        mlp_bank = [psum(f"mlp_bank{i}") for i in range(2)]

        idx_landed = [sem(f"idx_landed{u}") for u in range(U)]
        dense_landed = [sem(f"dense_landed{u}") for u in range(U)]
        rows_landed = [[sem(f"rows_landed{u}_{g}") for g in range(NGR)] for u in range(U)]
        ids_bc_landed = [sem(f"ids_bc_landed{half}") for half in range(2)]
        tbl_landed = [sem(f"tbl_landed{i}") for i in range(RAWS)]
        w1_landed = sem("w1_landed")
        w_pair_2_landed = sem("w_pair_2_landed")
        w2_landed = sem("w2_landed")
        vectors_landed = sem("vectors_landed")
        out_stored = sem("out_stored")
        ones_made = sem("ones_made")
        consts_made = sem("consts_made")
        pads_made = sem("pads_made")
        w_dense_made = sem("w_dense_made")
        w_hi_made = sem("w_hi_made")
        w_lo_made = sem("w_lo_made")
        hi_made = sem("hi_made")
        lo_made = sem("lo_made")
        onehot_made = sem("onehot_made")
        turned = sem("turned")
        picked = sem("picked")
        turn_copied = sem("turn_copied")
        dense_hi_made = sem("dense_hi_made")
        dense_lo_made = sem("dense_lo_made")
        gram_made = sem("gram_made")
        gram_copied = sem("gram_copied")
        post_made = sem("post_made")
        post_copied = sem("post_copied")
        pairs_hi_made = sem("pairs_hi_made")
        l1_made = sem("l1_made")
        h1_made = sem("h1_made")
        h1_lo_made = sem("h1_lo_made")
        l2_made = sem("l2_made")
        l2_read = sem("l2_read")
        y_made = sem("y_made")
        y_turned = sem("y_turned")
        y_rows_made = sem("y_rows_made")
        sp_passed = sem("sp_passed")
        pool_passed = sem("pool_passed")
        pe_passed = sem("pe_passed")

        block = ctx.enter_context(nc.Block())

        def load_table(engine, i):
            src = tables[TG + i].rearrange("(p c) d -> p c d", c=NCH)
            engine.dma_start(tbl_raw[i % RAWS][0:CR], src).then_inc(tbl_landed[i % RAWS], 16)

        def put_gram(copy, bank, u, h):
            src = bank[:].rearrange("p (k c) -> p c k", c=PAD)
            at = slice(u * K + h * SETS, u * K + (h + 1) * SETS)
            copy(gram[:, 0:CS, 0, at], src[:, 0:CS, :])
            copy(gram[:, :, 1, at], src[:, CS:F, :]).then_inc(gram_copied, 1)

        def pair_parts(i):
            bank = post_bank[(len(JGROUPS) + i) % 2]
            if i == 0:
                return [bank[0:FB, :].rearrange("p (s c j) -> p c s j", s=S, c=2)] + [
                    x[:, 0:2, :].rearrange("p c (s j) -> p c s j", s=S) for x in (pairs_hi, pairs_lo)]
            return [bank[0:FA - FB, 0:BS]] + [x[0:FA - FB, 2, :] for x in (pairs_hi, pairs_lo)]

        def l1_out(n, spread):
            if spread:
                return (turn_bank + mlp_bank[1:])[n][:, 0:BS]
            return mlp_bank[n // 2][:, (n % 2) * BS:(n % 2 + 1) * BS]

        @block.sync
        def _(sp):
            def load_idx(b, u):
                sp.dma_start(idx[u][:], ids[bass.ds(b * BS + u * P, P), :]).then_inc(idx_landed[u], 16)

            def load_dense(b, u):
                sp.dma_start(rows[u][:, 0, :],
                             dense[bass.ds(b * BS + u * P, P), :]).then_inc(dense_landed[u], 16)

            def load_ids_bc(b, half):
                at = slice(half * NOH // 2, (half + 1) * NOH // 2)
                src = ids_t[TG + at.start:TG + at.stop, bass.ds(b * BS, BS)].partition_broadcast(P)
                sp.dma_start(ids_bc[:, at, :], src).then_inc(ids_bc_landed[half], 16)

            load_idx(0, 0)
            load_ids_bc(0, 0)
            load_dense(0, 0)
            load_ids_bc(0, 1)
            load_idx(0, 1)
            for i in range(2, NOH):
                if i >= RAWS:
                    sp.wait_ge(lo_made, i - RAWS + 1)
                load_table(sp, i)
            load_dense(0, 1)
            sp.dma_start(w_pair_2, w1[D + CHUNKS[2][0]:D + CHUNKS[2][1], :]).then_inc(w_pair_2_landed, 16)
            sp.dma_start(w2_raw, w2.rearrange("(k p) n -> p k n", p=P)).then_inc(w2_landed, 16)

            def load_block(b, u):
                for g in range(NGR):
                    lo, hi = GROUPS[g]
                    sp.wait_ge(rows_landed[u][g], b * 16 * (hi - max(lo, 1)))
                    sp.sem_inc(sp_passed, 1)
                load_idx(b, u)
                sp.wait_ge(turned, (b - 1) * TILE_GROUPS + u * NGR + 1)
                load_dense(b, u)
                if u == 0:
                    for half in range(2):
                        sp.wait_ge(onehot_made, (b - 1) * NOH + (half + 1) * NOH // 2)
                        load_ids_bc(b, half)

            load_block(1, 0)
            sp.wait_ge(lo_made, NOH)
            sp.dma_start(w_dense, w1[0:D, :]).then_inc(w1_landed, 16)
            sp.dma_start(w_dense2, w1[D + NPAIR:2 * D + NPAIR, :]).then_inc(w1_landed, 16)
            for q, (lo, hi) in enumerate(CHUNKS[0:2]):
                sp.dma_start(w_pair_01[:, q, :], w1[D + lo:D + hi, :]).then_inc(w1_landed, 16)
            sp.dma_start(b1_sb[:], b1).then_inc(vectors_landed, 16)
            sp.dma_start(b2_bc[:], b2.partition_broadcast(P)).then_inc(vectors_landed, 16)
            sp.dma_start(w3_bc[:], w3.partition_broadcast(P)).then_inc(vectors_landed, 16)
            load_block(1, 1)
            with sp.Fori(2, NB) as b:
                for u in range(U):
                    load_block(b, u)

        @block.gpsimd
        def _(pool):
            nc.gpsimd.memset(ones[:], 1.0).then_inc(ones_made, 1)
            pool.wait_ge(ones_made, 1)
            nc.gpsimd.affine_select(out=ident[:], in_=ones[:], compare_op=ALU.is_equal, fill=0.0, base=0,
                                    pattern=[[-1, P]], channel_multiplier=1).then_inc(consts_made, 1)
            nc.gpsimd.iota(row_of[:], pattern=[[1, NCH]], base=0, channel_multiplier=NCH).then_inc(consts_made, 1)

            def gather(b, first):
                for u in range(U):
                    pool.wait_ge(idx_landed[u], (b + 1) * 16)
                    for g, (lo, hi) in enumerate(GROUPS):
                        if not first:
                            pool.wait_ge(turned, (b - 1) * TILE_GROUPS + u * NGR + g + 1)
                            pool.sem_inc(pool_passed, 1)
                        for slot in range(max(lo, 1), hi):
                            t = slot - 1
                            nc.gpsimd.indirect_dma_start(
                                rows[u][:, slot, :], None, tables[t],
                                bass.IndirectOffsetOnAxis(ap=idx[u][:, t:t + 1], axis=0),
                            ).then_inc(rows_landed[u][g], 16)

            gather(0, True)
            with pool.Fori(1, NB) as b:
                gather(b, False)

        @block.tensor
        def _(pe):
            def turn_tile(b, u, first, groups=range(NGR)):
                for g in groups:
                    lo, hi = GROUPS[g]
                    n = turn_use[u, g]
                    if lo == 0:
                        pe.wait_ge(dense_landed[u], (b + 1) * 16)
                    pe.wait_ge(rows_landed[u][g], (b + 1) * 16 * (hi - max(lo, 1)))
                    if not first or n >= TB:
                        pe.wait_ge(turn_copied, (b - 1) * TURNS + last_use(n, TURNS, TB))
                    for slot in range(lo, hi):
                        j = slot - lo
                        mm = nc.tensor.transpose(turn_bank[n % TB][:, j * P:(j + 1) * P],
                                                 rows[u][:, slot, :], ident[:])
                    mm.then_inc(turned, 1)

            def pick(b, first, groups=range(NOG)):
                for g in groups:
                    lo, hi = OGROUPS[g]
                    n = turn_use["oh", g]
                    if not first or n >= TB:
                        pe.wait_ge(turn_copied, (b - 1) * TURNS + last_use(n, TURNS, TB))
                    for i in range(lo, hi):
                        pe.wait_ge(onehot_made, b * NOH + i + 1)
                        if first:
                            pe.wait_ge(lo_made, i + 1)
                        for c in range(NCH):
                            for part in (tbl_hi, tbl_lo):
                                mm = nc.tensor.matmul(
                                    turn_bank[n % TB][:, (i - lo) * BS:(i - lo + 1) * BS],
                                    part[i][0:CR, c, :], onehot[i % OH_BUFS][0:CR, c, :],
                                    start=(c == 0 and part is tbl_hi), stop=(c == NCH - 1 and part is tbl_lo))
                        mm.then_inc(picked, 1)

            def gram_tile(b, u, first, banks=range(GB), bank=gram_bank):
                pe.wait_ge(turn_copied, b * TURNS + (TURNS if u else TURNED_0))
                for h in banks:
                    if bank is gram_bank and (not first or u or h):
                        pe.wait_ge(gram_copied, (b * U + u) * GB + h)
                    for k in range(SETS):
                        for s in range(S):
                            at = s * K + h * SETS + k
                            mm = nc.tensor.matmul(bank[s * PAD:(s + 1) * PAD, k * PAD:k * PAD + F],
                                                  slot_flat[:, u, at * (F + 1):at * (F + 1) + PAD],
                                                  slot_t[:, u, at, 0:F],
                                                  start=True, stop=True, tile_position=(0, s * PAD))
                    mm.then_inc(gram_made, 1)

            def turn_gram(b, first, groups=range(len(JGROUPS))):
                for n in groups:
                    lo, hi = JGROUPS[n]
                    if n == 0:
                        pe.wait_ge(gram_copied, (b + 1) * U * GB)
                    if not first or n >= 2:
                        pe.wait_ge(post_copied, (b - 1) * POSTS + last_use(n, POSTS, 2))
                        pe.sem_inc(pe_passed, 1)
                    for j in range(lo, hi):
                        mm = nc.tensor.transpose(post_bank[n % 2][:, (j - lo) * P:(j - lo + 1) * P],
                                                 gram_flat[:, j * P:(j + 1) * P], ident[:])
                    mm.then_inc(post_made, 1)

            def turn_pairs(b):
                n = len(JGROUPS)
                pe.wait_ge(post_copied, b * POSTS + n)
                pe.sem_inc(pe_passed, 1)
                for s in range(S):
                    mm = nc.tensor.transpose(post_bank[n % 2][0:FB, s * P:(s + 1) * P],
                                             pairs[:, s, 0:FB], ident[:])
                mm.then_inc(post_made, 1)
                for s in range(S):
                    at = s * U * K
                    mm = nc.tensor.transpose(post_bank[(n + 1) % 2][0:FA - FB, at:at + U * K],
                                             pairs[0:U * K, s, FB:FA], ident[0:U * K, 0:U * K])
                mm.then_inc(post_made, 1)

            def split_product(dst, w_hi, w_lo, x_hi, x_lo, start, stop):
                nc.tensor.matmul(dst, w_hi, x_hi, start=start, stop=False)
                nc.tensor.matmul(dst, w_hi, x_lo, start=False, stop=False)
                return nc.tensor.matmul(dst, w_lo, x_hi, start=False, stop=stop)

            def layer1(b, first, parts=range(N1), spread=False):
                if first:
                    pe.wait_ge(w_lo_made, 4)
                pe.wait_ge(dense_lo_made, b + 1)
                pe.wait_ge(post_copied, (b + 1) * POSTS)
                for n in parts:
                    if not first and not spread and n % 2 == 0:
                        pe.wait_ge(l2_read, (b - 1) * U + n // 2 + 1)
                    if spread and n == N1 - 1:
                        pe.wait_ge(l2_read, b * U)
                    dst = l1_out(n, spread)
                    at = slice(n * P, (n + 1) * P)
                    split_product(dst, w_dense_hi[:, at], w_dense_lo[:, at], dense_hi[:], dense_lo[:], True, False)
                    for q, (lo, hi) in enumerate(CHUNKS):
                        mm = split_product(dst, w_pair_hi[0:hi - lo, q, at], w_pair_lo[0:hi - lo, q, at],
                                           pairs_hi[0:hi - lo, q, :], pairs_lo[0:hi - lo, q, :], False, q == 2)
                    mm.then_inc(l1_made, 1)

            def layer2(b, tiles=range(U)):
                for u in tiles:
                    at = slice(u * P, (u + 1) * P)
                    for k in range(N1):
                        if u == 0:
                            pe.wait_ge(h1_lo_made, b * N1 + max(k, 1) + 1)
                        mm = split_product(mlp_bank[u][:, 0:H2], h1_hi[:, k, at], h1_lo[:, k, at],
                                           w2_hi[:, k, :], w2_lo[:, k, :], k == 0, k == N1 - 1)
                    mm.then_inc(l2_made, 1)

            pe.wait_ge(consts_made, 1)
            turn_tile(0, 0, True, range(0, 1))
            pick(0, True, range(0, 1))
            turn_tile(0, 0, True, range(1, 3))
            pick(0, True, range(1, 3))
            turn_tile(0, 0, True, range(3, NGR - 1))
            pick(0, True, range(3, NOG))
            turn_tile(0, 0, True, range(NGR - 1, NGR))
            turn_tile(0, 1, True, range(0, 1))
            pe.wait_ge(pads_made, 1)
            gram_tile(0, 0, True, range(0, 1))
            turn_tile(0, 1, True, range(1, 3))
            gram_tile(0, 0, True, range(1, GB))
            turn_tile(0, 1, True, range(3, NGR))
            gram_tile(0, 1, True, range(0, 1))

            def first_half(b, second):
                turn_tile(b, 0, False, range(0, 1))
                pick(b, False, range(0, 1))
                gram_tile(b - 1, 1, second, range(1, GB))
                turn_tile(b, 0, False, range(1, 3))
                turn_gram(b - 1, second, range(0, 2))
                pick(b, False, range(1, 3))
                turn_tile(b, 0, False, range(3, NGR - 1))
                turn_gram(b - 1, second, range(2, len(JGROUPS)))
                pick(b, False, range(3, NOG))
                turn_tile(b, 0, False, range(NGR - 1, NGR))
                turn_pairs(b - 1)
                turn_tile(b, 1, False, range(0, 1))
                gram_tile(b, 0, False, range(0, 1))

            def body(b, second):
                first_half(b, second)
                layer1(b - 1, second)
                gram_tile(b, 0, False, range(1, GB))
                turn_tile(b, 1, False, range(1, 3))
                layer2(b - 1, range(0, 1))
                turn_tile(b, 1, False, range(3, NGR))
                layer2(b - 1, range(1, U))
                gram_tile(b, 1, False, range(0, 1))

            body(1, True)
            with pe.Fori(2, NB - 1) as b:
                body(b, False)

            last = NB - 1
            first_half(last, False)
            turn_tile(last, 1, False, range(1, 3))
            gram_tile(last, 0, False, range(1, GB))
            layer1(last - 1, False, range(0, 1))
            turn_tile(last, 1, False, range(3, NGR - 1))
            layer1(last - 1, False, range(1, 3))
            turn_tile(last, 1, False, range(NGR - 1, NGR))
            layer1(last - 1, False, range(3, N1))
            gram_tile(last, 1, False, range(0, 1))
            gram_tile(last, 1, False, range(1, GB), turn_bank[0])
            layer2(last - 1, range(0, 1))
            turn_gram(last, False, range(0, 2))
            layer2(last - 1, range(1, U))
            turn_gram(last, False, range(2, len(JGROUPS)))
            turn_pairs(last)
            layer1(last, False, spread=True)
            layer2(last)
            pe.wait_ge(y_made, NB * U)
            nc.tensor.transpose(post_bank[0][0:NB * U, 0:P], y_cols[:], ident[:]).then_inc(y_turned, 1)

        @block.scalar
        def _(act):
            def copy_tile(b, u, first, groups=range(NGR)):
                if not first and 0 in groups:
                    act.wait_ge(gram_made, ((b - 1) * U + u + 1) * GB)
                    act.wait_ge(dense_lo_made, b)
                for g in groups:
                    lo, hi = GROUPS[g]
                    n = turn_use[u, g]
                    act.wait_ge(turned, b * TILE_GROUPS + u * NGR + g + 1)
                    src = turn_bank[n % TB][:, 0:(hi - lo) * P].rearrange("d (f j) -> d j f", j=P)
                    nc.scalar.copy(slot_t[:, u, :, lo:hi], src).then_inc(turn_copied, 1)

            def copy_picked(b, first, groups):
                if not first and 0 in groups:
                    act.wait_ge(gram_made, b * U * GB)
                for g in groups:
                    lo, hi = OGROUPS[g]
                    n = turn_use["oh", g]
                    act.wait_ge(picked, b * NOH + hi)
                    dst = slot_t[:, :, :, NG + lo:NG + hi]
                    src = turn_bank[n % TB][:, 0:(hi - lo) * BS].rearrange("d (f u j) -> d u j f", u=U, j=P)
                    nc.scalar.copy(dst, src).then_inc(turn_copied, 1)

            def copy_dense(b, first):
                act.wait_ge(turn_copied, b * TURNS + turn_use[1, 0] + 1)
                if not first:
                    act.wait_ge(l1_made, b * N1)
                src = slot_t[:, :, :, 0].rearrange("d u (s k) -> d s u k", s=S)
                dst = dense_hi[:].rearrange("d (s u k) -> d s u k", s=S, u=U)
                nc.scalar.copy(dst, src).then_inc(dense_hi_made, 1)

            def copy_last_gram(b, bank=gram_bank):
                act.wait_ge(gram_made, (b + 1) * U * GB)
                put_gram(nc.scalar.copy, bank, U - 1, GB - 1)

            def relu1(b, parts=range(N1), spread=False):
                for n in parts:
                    if n % 2 == 0 or spread:
                        act.wait_ge(l1_made, b * N1 + (n + 1 if spread else n + 2))
                    src = l1_out(n, spread).rearrange("p (s u k) -> p s u k", s=S, u=U)
                    dst, dst_hi = (x[:, n, :].rearrange("p (u s k) -> p s u k", s=S, u=U) for x in (h1, h1_hi))
                    nc.scalar.activation(dst, src, ACT.Relu, bias=b1_sb[:, n:n + 1])
                    nc.scalar.activation(dst_hi, src, ACT.Relu, bias=b1_sb[:, n:n + 1]).then_inc(h1_made, 1)

            load_table(act, 0)
            load_table(act, 1)

            def split_table(i):
                act.wait_ge(tbl_landed[i % RAWS], (i // RAWS + 1) * 16)
                nc.scalar.copy(tbl_hi[i][0:CR], tbl_raw[i % RAWS][0:CR]).then_inc(hi_made, 1)

            split_table(0)
            split_table(1)
            split_table(2)
            copy_tile(0, 0, True, range(0, 1))
            split_table(3)
            split_table(4)
            copy_picked(0, True, range(0, 1))
            copy_tile(0, 0, True, range(1, 2))
            split_table(5)
            copy_tile(0, 0, True, range(2, 3))
            copy_picked(0, True, range(1, 2))
            for i in range(6, NOH):
                split_table(i)
            copy_picked(0, True, range(2, 3))
            copy_tile(0, 0, True, range(3, NGR - 1))
            act.wait_ge(w_pair_2_landed, 16)
            nc.scalar.copy(w_pair_hi[0:FA - FB, 2, :], w_pair_2).then_inc(w_hi_made, 1)
            act.wait_ge(w2_landed, 16)
            nc.scalar.copy(w2_hi[:], w2_raw).then_inc(w_hi_made, 1)
            copy_picked(0, True, range(3, NOG))
            copy_tile(0, 0, True, range(NGR - 1, NGR))
            copy_tile(0, 1, True)
            copy_dense(0, True)
            act.wait_ge(w_dense_made, 1)
            nc.scalar.copy(w_dense_hi[:], w_dense).then_inc(w_hi_made, 1)
            nc.scalar.copy(w_pair_hi[:, 0:2, :], w_pair_01).then_inc(w_hi_made, 1)

            def first_half(b):
                copy_tile(b, 0, False, range(0, 1))
                copy_last_gram(b - 1)
                copy_picked(b, False, range(0, 1))
                copy_tile(b, 0, False, range(1, 3))
                copy_picked(b, False, range(1, 3))
                copy_tile(b, 0, False, range(3, NGR - 1))
                copy_picked(b, False, range(3, NOG))
                copy_tile(b, 0, False, range(NGR - 1, NGR))
                copy_tile(b, 1, False, range(0, 1))

            def body(b):
                first_half(b)
                relu1(b - 1)
                copy_tile(b, 1, False, range(1, NGR))
                copy_dense(b, False)

            act.wait_ge(w_lo_made, 4)
            act.wait_ge(vectors_landed, 3 * 16)
            with act.Fori(1, NB - 1) as b:
                body(b)

            last = NB - 1
            first_half(last)
            copy_tile(last, 1, False, range(1, NGR - 1))
            relu1(last - 1, range(0, 2))
            copy_tile(last, 1, False, range(NGR - 1, NGR))
            relu1(last - 1, range(2, N1))
            copy_dense(last, False)
            copy_last_gram(last, turn_bank[0])
            for i in range(2):
                act.wait_ge(post_made, last * POSTS + len(JGROUPS) + i + 1)
                src, hi, _ = pair_parts(i)
                nc.scalar.copy(hi, src).then_inc(pairs_hi_made, 1)
            relu1(last, spread=True)
            act.wait_ge(y_turned, 1)
            nc.scalar.copy(y_rows[:], post_bank[0][0:NB * U, 0:P]).then_inc(y_rows_made, 1)
            act.wait_ge(y_rows_made, 1)
            act.dma_start(out.rearrange("(n j) o -> n (j o)", j=P), y_rows[:]).then_inc(out_stored, 16)
            act.wait_ge(out_stored, 16)

        @block.vector
        def _(dve):
            def make_onehot(b, i, first):
                if i in (0, NOH // 2):
                    dve.wait_ge(ids_bc_landed[2 * i // NOH], (b + 1) * 16)
                if not first or i >= OH_BUFS:
                    dve.wait_ge(picked, (b - 1) * NOH + last_use(i, NOH, OH_BUFS))
                nc.vector.tensor_tensor(
                    onehot[i % OH_BUFS][0:CR], ids_bc[0:CR, i:i + 1, :].to_broadcast([CR, NCH, BS]),
                    row_of[0:CR, :].unsqueeze(2).to_broadcast([CR, NCH, BS]), ALU.is_equal,
                ).then_inc(onehot_made, 1)

            def copy_gram(b, u, h):
                dve.wait_ge(gram_made, (b * U + u) * GB + h + 1)
                put_gram(nc.vector.tensor_copy, gram_bank, u, h)

            def pack_pairs(b, groups=range(len(JGROUPS))):
                for n in groups:
                    lo, hi = JGROUPS[n]
                    dve.wait_ge(post_made, b * POSTS + n + 1)
                    for j in range(lo, hi):
                        for part, c in enumerate((j, CS + j)):
                            if part == 0 and c >= CS:
                                continue
                            at = slice(part * U * K, (part + 1) * U * K)
                            src = post_bank[n % 2][at, (j - lo) * P:(j - lo + 1) * P]
                            src = src.rearrange("p (s a) -> p s a", a=PAD)[:, :, c + 1:F + 1]
                            dst = pairs[at, :, pair_at[c] - part * FA:pair_at[c + 1] - part * FA]
                            cp = nc.vector.tensor_copy(dst, src)
                    cp.then_inc(post_copied, 1)

            def split_pairs(b, high=True):
                for i in range(2):
                    dve.wait_ge(post_made, b * POSTS + len(JGROUPS) + i + 1)
                    src, hi, lo = pair_parts(i)
                    if high:
                        nc.vector.tensor_copy(hi, src).then_inc(pairs_hi_made, 1)
                    dve.wait_ge(pairs_hi_made, b * 2 + i + 1)
                    nc.vector.tensor_tensor(lo, src, hi.bitcast(F32), ALU.subtract).then_inc(post_copied, 1)

            def split_dense(b):
                dve.wait_ge(dense_hi_made, b + 1)
                nc.vector.tensor_tensor(
                    dense_lo[:].rearrange("d (s u k) -> d s u k", s=S, u=U),
                    slot_t[:, :, :, 0].rearrange("d u (s k) -> d s u k", s=S),
                    dense_hi[:].bitcast(F32).rearrange("d (s u k) -> d s u k", s=S, u=U),
                    ALU.subtract).then_inc(dense_lo_made, 1)

            def split_h1(b, parts=range(N1)):
                for n in parts:
                    dve.wait_ge(h1_made, b * N1 + n + 1)
                    nc.vector.tensor_tensor(h1_lo[:, n, :], h1[:, n, :], h1_hi[:, n, :].bitcast(F32),
                                            ALU.subtract).then_inc(h1_lo_made, 1)

            def layer3(b, u):
                dve.wait_ge(l2_made, b * U + u + 1)
                nc.vector.tensor_tensor(h2[:, u, :], mlp_bank[u][:, 0:H2], b2_bc[:], ALU.add).then_inc(l2_read, 1)
                dve.wait_ge(l2_read, b * U + u + 1)
                nc.vector.scalar_tensor_tensor(
                    h2[:, u, :], h2[:, u, :], 0.0, w3_bc[:], ALU.max, ALU.mult,
                    accum_out=y_cols[:, bass.ds(b * U + u, 1)]).then_inc(y_made, 1)

            nc.vector.memset(slot_flat[:, :, P * (F + 1):], 0.0).then_inc(pads_made, 1)
            nc.vector.memset(gram[:, CS:, 0, :], 0.0)
            dve.wait_ge(consts_made, 2)
            for i in range(NOH):
                dve.wait_ge(hi_made, i + 1)
                nc.vector.tensor_tensor(tbl_lo[i][0:CR], tbl_raw[i % RAWS][0:CR],
                                        tbl_hi[i][0:CR].bitcast(F32), ALU.subtract).then_inc(lo_made, 1)
                make_onehot(0, i, True)

            def split_weight(i, lo, hi, whole):
                dve.wait_ge(w_hi_made, i + 1)
                nc.vector.tensor_tensor(lo, whole, hi.bitcast(F32), ALU.subtract).then_inc(w_lo_made, 1)

            split_weight(0, w_pair_lo[0:FA - FB, 2, :], w_pair_hi[0:FA - FB, 2, :], w_pair_2)
            split_weight(1, w2_lo[:], w2_hi[:], w2_raw)
            copy_gram(0, 0, 0)
            make_onehot(1, 0, False)
            copy_gram(0, 0, 1)
            make_onehot(1, 1, False)
            dve.wait_ge(w1_landed, 4 * 16)
            nc.vector.tensor_tensor(w_dense, w_dense, w_dense2, ALU.add).then_inc(w_dense_made, 1)
            make_onehot(1, 2, False)
            split_dense(0)
            copy_gram(0, 1, 0)
            split_weight(2, w_dense_lo[:], w_dense_hi[:], w_dense)
            split_weight(3, w_pair_lo[:, 0:2, :], w_pair_hi[:, 0:2, :], w_pair_01)

            def first_half(b):
                make_onehot(b, OH_BUFS, False)
                make_onehot(b, OH_BUFS + 1, False)
                pack_pairs(b - 1, range(0, 1))
                make_onehot(b, OH_BUFS + 2, False)
                pack_pairs(b - 1, range(1, 2))
                for i in range(OH_BUFS + 3, NOH):
                    make_onehot(b, i, False)
                pack_pairs(b - 1, range(2, len(JGROUPS)))
                split_pairs(b - 1)
                copy_gram(b, 0, 0)

            dve.wait_ge(vectors_landed, 3 * 16)
            with dve.Fori(1, NB - 1) as b:
                first_half(b)
                split_h1(b - 1)
                copy_gram(b, 0, 1)
                make_onehot(b + 1, 0, False)
                layer3(b - 1, 0)
                make_onehot(b + 1, 1, False)
                layer3(b - 1, 1)
                split_dense(b)
                copy_gram(b, 1, 0)
                make_onehot(b + 1, 2, False)

            last = NB - 1
            first_half(last)
            copy_gram(last, 0, 1)
            split_h1(last - 1)
            split_dense(last)
            copy_gram(last, 1, 0)
            pack_pairs(last)
            layer3(last - 1, 0)
            split_pairs(last, high=False)
            layer3(last - 1, 1)
            split_h1(last)
            for u in range(U):
                layer3(last, u)


def kernel(**inputs):
    import numpy as _np
    import concourse.bacc as _bacc
    from concourse import mybir as _mybir
    from concourse.bass_utils import run_bass_kernel_spmd as _run

    nc = _bacc.Bacc("TRN2", target_bir_lowering=False, num_devices=1)
    arrays = {}

    def given(name, array):
        a = _np.ascontiguousarray(array)
        arrays[f"in_{name}_dram"] = a
        return nc.dram_tensor(f"in_{name}_dram", a.shape, _mybir.dt.from_np(a.dtype), kind="ExternalInput").ap()

    dense = given("r_dense_features", inputs["r_dense_features"])
    ids = given("ids", inputs["ids"])
    ids_t = given("ids_t", _np.asarray(inputs["ids"]).T)
    tables = [given(f"tbl_{t}", inputs[f"tbl_{t}"]) for t in range(inputs["ids"].shape[1])]
    w1, w2 = given("W_top1", inputs["W_top1"]), given("W_top2", inputs["W_top2"])
    b1 = given("b_top1", _np.asarray(inputs["b_top1"]).reshape(-1, 128).T)
    b2, w3 = (given(n, _np.asarray(inputs[n]).reshape(-1)) for n in ("b_top2", "W_top3"))
    out = nc.dram_tensor("out_0_dram", (dense.shape[0], 1), _mybir.dt.float32, kind="ExternalOutput").ap()
    build_dlrm_tower(nc, dense, ids, ids_t, tables, w1, b1, w2, b2, w3, out)
    r = _run(nc, [arrays], core_ids=[0])
    return r.results[0]["out_0_dram"]
```
